# Optimizing a Trainium2 kernel written in Bass

```python
import numpy as np
import jax
import jax.numpy as jnp

def _softmax(x, axis=-1):
    return jax.nn.softmax(x, axis=axis)

def _gelu(x):
    return jax.nn.gelu(x, approximate=True)

def _silu(x):
    return jax.nn.silu(x)

def _sigmoid(x):
    return jax.nn.sigmoid(x)

def _layernorm(x, axis=-1, eps=1e-05):
    m = jnp.mean(x, axis=axis, keepdims=True)
    v = jnp.var(x, axis=axis, keepdims=True)
    return (x - m) / jnp.sqrt(v + eps)

def _scatter_add(tgt, idx, src, axis=0):
    return tgt.at[idx].add(src)

def _segment_sum(src, seg, n):
    return jax.ops.segment_sum(src, seg, n)
kernel_name = 'mk_gnn_resnorm_d2_gnn_r8_612c65'

def setup_inputs(seed: int=0):
    np.random.seed(seed)
    _w = jnp.asarray

    def _rec_inputs():
        import jax
        import jax.numpy as jnp
        _gk = jax.random.key(seed)
        x = -0.0001006 + 1 * jax.random.normal(jax.random.fold_in(_gk, 1), (12500, 96), jnp.float32)
        src = jax.random.randint(jax.random.fold_in(_gk, 2), (400000,), 0, 12500, jnp.int32)
        dst = jnp.minimum((12500 * jax.random.uniform(jax.random.fold_in(_gk, 3), (400000,)) ** 2.0).astype(jnp.int32), 99999)
        _o = jnp.argsort(dst, stable=True)
        src = src[_o]
        dst = dst[_o]
        edge_attr_32 = 0.000196303 + 1.00016 * jax.random.normal(jax.random.fold_in(_gk, 11), (400000, 32), jnp.float32)
        return (x, src, dst, edge_attr_32)
    x, src, dst, edge_attr_32 = _rec_inputs()

    def _L0_gnn_setup():
        import jax, jax.numpy as jnp
        import numpy as np
        N_NODES = 6250
        N_EDGES = 100000
        IN_DIM = 96
        OUT_DIM = 96
        EDGE_DIM = 32
        BN_EPS = 1e-05
        key = jax.random.key(seed)
        ks = jax.random.split(key, 12)
        x = jax.random.normal(ks[0], (N_NODES, IN_DIM), dtype=jnp.float32)
        edge_index = jax.random.randint(ks[1], (2, N_EDGES), 0, N_NODES, dtype=jnp.int64)
        edge_attr = jax.random.normal(ks[2], (N_EDGES, EDGE_DIM), dtype=jnp.float32)
        We = jax.random.normal(ks[3], (EDGE_DIM, IN_DIM), dtype=jnp.float32) / np.sqrt(EDGE_DIM)
        be = jnp.zeros((IN_DIM,), dtype=jnp.float32)
        W1 = jax.random.normal(ks[4], (IN_DIM, OUT_DIM), dtype=jnp.float32) / np.sqrt(IN_DIM)
        b1 = jnp.zeros((OUT_DIM,), dtype=jnp.float32)
        W2 = jax.random.normal(ks[5], (OUT_DIM, OUT_DIM), dtype=jnp.float32) / np.sqrt(OUT_DIM)
        b2 = jnp.zeros((OUT_DIM,), dtype=jnp.float32)
        gamma = jnp.ones((OUT_DIM,), dtype=jnp.float32)
        beta = jnp.zeros((OUT_DIM,), dtype=jnp.float32)
        return {'x': x, 'edge_index': edge_index, 'edge_attr': edge_attr, 'We': We, 'be': be, 'W1': W1, 'b1': b1, 'W2': W2, 'b2': b2, 'gamma': gamma, 'beta': beta}
    _L0_gnn_all = _L0_gnn_setup()
    _L0_gnn_in = {k: v for k, v in _L0_gnn_all.items() if k in ('We', 'be', 'W1', 'b1', 'W2', 'b2', 'gamma', 'beta')}
    del _L0_gnn_all

    def _L1_gnn_setup():
        import jax, jax.numpy as jnp
        import numpy as np
        N_NODES = 6250
        N_FEAT = 96
        N_EDGES = 100000
        K_HOPS = 2
        key = jax.random.key(seed)
        k1, k2 = jax.random.split(key)
        x = jax.random.normal(k1, (N_NODES, N_FEAT), dtype=jnp.float32)
        edge_index = jax.random.randint(k2, (2, N_EDGES), 0, N_NODES, dtype=jnp.int64)
        return {'x': x, 'edge_index': edge_index}
    _L1_gnn_all = _L1_gnn_setup()
    _L1_gnn_in = {k: v for k, v in _L1_gnn_all.items() if k in ()}
    del _L1_gnn_all
    return {'x': x, 'src': src, 'dst': dst, 'edge_attr_32': edge_attr_32, 'L0_gnn_We': _L0_gnn_in['We'], 'L0_gnn_be': _L0_gnn_in['be'], 'L0_gnn_W1': _L0_gnn_in['W1'], 'L0_gnn_b1': _L0_gnn_in['b1'], 'L0_gnn_W2': _L0_gnn_in['W2'], 'L0_gnn_b2': _L0_gnn_in['b2'], 'L0_gnn_gamma': _L0_gnn_in['gamma'], 'L0_gnn_beta': _L0_gnn_in['beta']}

def reference(x, src, dst, edge_attr_32, L0_gnn_We, L0_gnn_be, L0_gnn_W1, L0_gnn_b1, L0_gnn_W2, L0_gnn_b2, L0_gnn_gamma, L0_gnn_beta):
    import jax
    import jax.numpy as jnp

    def _L0_gnn_ref(x, edge_index, edge_attr, We, be, W1, b1, W2, b2, gamma, beta):
        import jax, jax.numpy as jnp
        import numpy as np
        N_NODES = 6250
        N_EDGES = 100000
        IN_DIM = 96
        OUT_DIM = 96
        EDGE_DIM = 32
        BN_EPS = 1e-05
        src = edge_index[0]
        dst = edge_index[1]
        msg = jax.nn.relu(x[src] + edge_attr @ We + be)
        aggr = jax.ops.segment_sum(msg, dst, num_segments=x.shape[0])
        h = x + aggr
        h = jax.nn.relu(h @ W1 + b1) @ W2 + b2
        mean = jnp.mean(h, axis=0)
        var = jnp.mean(jnp.square(h - mean), axis=0)
        h = (h - mean) * jax.lax.rsqrt(var + BN_EPS) * gamma + beta
        return jax.nn.relu(h)

    def _L1_gnn_ref(x, edge_index):
        import jax, jax.numpy as jnp
        import numpy as np
        N_NODES = 6250
        N_FEAT = 96
        N_EDGES = 100000
        K_HOPS = 2
        N = x.shape[0]
        loops = jnp.arange(N, dtype=edge_index.dtype)
        src = jnp.concatenate([edge_index[0], loops])
        dst = jnp.concatenate([edge_index[1], loops])
        ew = jnp.ones(src.shape[0], dtype=x.dtype)
        deg = jax.ops.segment_sum(ew, dst, num_segments=N)
        deg_inv_sqrt = jnp.where(deg > 0, jax.lax.rsqrt(deg), jnp.zeros_like(deg))
        norm = deg_inv_sqrt[src] * ew * deg_inv_sqrt[dst]

        def hop(h):
            return jax.ops.segment_sum(norm[:, None] * h[src], dst, num_segments=N)
        h = x
        for _ in range(K_HOPS):
            h = hop(h)
        return h
    edge_index = jnp.stack([src, dst])
    x = _layernorm(x + _L0_gnn_ref(x, edge_index, edge_attr_32, L0_gnn_We, L0_gnn_be, L0_gnn_W1, L0_gnn_b1, L0_gnn_W2, L0_gnn_b2, L0_gnn_gamma, L0_gnn_beta), axis=-1)
    x = _layernorm(x + _L1_gnn_ref(x, edge_index), axis=-1)
    return x

_drawn_inputs = setup_inputs


def setup_inputs(seed=0):
    import zlib

    import numpy as np

    out = dict(_drawn_inputs(seed))
    spreads = {'L0_gnn_be': (0.0, 0.1),
     'L0_gnn_b1': (0.0, 2.0),
     'L0_gnn_b2': (0.0, 2.0),
     'L0_gnn_gamma': (1.0, 0.2),
     'L0_gnn_beta': (0.0, 0.1)}
    factors = {}
    for name, (base, spread) in spreads.items():
        noise = np.random.default_rng([zlib.crc32(name.encode()), seed]).standard_normal(out[name].shape)
        drawn = base * np.exp(spread * noise) if base else spread * noise
        out[name] = jnp.asarray(drawn.astype(out[name].dtype))
    for name, factor in factors.items():
        out[name] = (out[name] * factor).astype(out[name].dtype)
    return out
```

```python
from contextlib import ExitStack

import concourse.bass as bass
from concourse import mybir

F32 = mybir.dt.float32
I32 = mybir.dt.int32
U32 = mybir.dt.uint32
ALU = mybir.AluOpType
ACT = mybir.ActivationFunctionType
AX_X = mybir.AxisListType.X

P = 128
EPS = 1e-5


def gnn_kernel(nc, x, src, dst, ea, We, be, W1, b1, W2, b2, gamma, beta, out):
    N, F = x.shape
    E, D = ea.shape
    WINDOWS = -(-N // P)
    TAIL = N - (WINDOWS - 1) * P
    G = 5
    SUPER = G * P
    SUPERS = E // SUPER
    RING = 5
    TURNS = SUPERS // RING
    ROWS = SUPERS // RING
    assert E % (SUPER * RING) == 0 and ROWS <= P and 4 * D == P and F * G <= 512
    FD = F + 1
    GROUP = 4
    GROUPS = -(-WINDOWS // GROUP)
    GN = GROUP * P
    LAST = WINDOWS - (GROUPS - 1) * GROUP
    BN = 500
    assert N % BN == 0 and GROUPS % 2 == 1

    xb_dram = nc.dram_tensor("xb_scratch", (WINDOWS * P, F), F32, kind="Internal").ap()
    g_dram = [nc.dram_tensor(f"g{h}_scratch", (WINDOWS * P, F), F32, kind="Internal").ap() for h in range(2)]
    span_dram = nc.dram_tensor("span_scratch", (SUPERS * 2,), I32, kind="Internal").ap()

    with ExitStack() as ctx:
        def sb(name, shape, dt=F32):
            return ctx.enter_context(nc.sbuf_tensor(name, shape, dt))

        def sem(name):
            return ctx.enter_context(nc.semaphore(name))

        bank = [ctx.enter_context(nc.psum_tensor(f"bank{i}", [P, 512], F32)) for i in range(8)]
        eaT_ps, seg_ps = bank[0], bank[3]
        emb_ps = [bank[1], bank[2]]

        ident = sb("ident", [P, P])
        node_i = sb("node_i", [P, P], I32)
        node = sb("node", [P, P])
        base_i = sb("base_i", [P, WINDOWS], I32)
        base = sb("base", [P, WINDOWS])
        eps = sb("eps", [P, 1])
        wide = sb("wide", [P, 4 * RING * SUPER])
        raw = {n: wide[0:ROWS, i * RING * SUPER:(i + 1) * RING * SUPER].bitcast(I32) for i, n in enumerate(("src", "dst"))}
        flt = {n: wide[0:ROWS, (2 + i) * RING * SUPER:(3 + i) * RING * SUPER] for i, n in enumerate(("src", "dst"))}
        h2T = wide[0:F, 0:WINDOWS * P]
        src_all = sb("src_all", [P, (SUPERS + RING) * G], U32)
        dst_all = sb("dst_all", [P, SUPERS * G])
        span_f = sb("span_f", [ROWS, RING, 2])
        span_n = sb("span_n", [ROWS, RING, 2], I32)
        span_w = sb("span_w", [ROWS, RING, 2], I32)
        span = sb("span", [1, SUPERS * 2], I32)
        xs = sb("xs", [P, WINDOWS * F])
        agg = sb("agg", [P, WINDOWS * FD])
        dis = sb("dis", [P, WINDOWS])
        inv = sb("inv", [P, WINDOWS])
        deg = sb("deg", [P, WINDOWS])
        root = sb("root", [P, WINDOWS])
        be_all = sb("be_all", [P, F])
        We4 = sb("We4", [P, 4 * F])
        W1_sb = sb("W1_sb", [F, F])
        W2_sb = sb("W2_sb", [F, F])
        cols = sb("cols", [F, 4])
        idx = sb("idx", [P, RING * G], U32)
        rows = sb("rows", [P, RING, G * F])
        ea_sb = sb("ea_sb", [P, RING, G * D])
        eaT = sb("eaT", [P, 2 * P])
        msg = sb("msg", [P, G * FD])
        hot = sb("hot", [P, SUPER])
        hs = sb("hs", [P, GROUP, F])
        yT = sb("yT", [F, GN])
        hT = sb("hT", [F, GN])
        hid = sb("hid", [F, GN])
        stats = sb("stats", [F, N // BN, 6])
        mv = sb("mv", [F, 2])
        bn = sb("bn", [F, 4])
        bnt = sb("bnt", [F, 1])
        lst = sb("lst", [P, GROUP, 6])
        lmv = sb("lmv", [P, GROUP, 2])
        lroot = sb("lroot", [P, GROUP])
        lrs = sb("lrs", [P, GROUP])

        agg3 = agg[:, :].rearrange("p (w f) -> p w f", f=FD)
        xs3 = xs[:, :].rearrange("p (w f) -> p w f", f=F)
        msg3 = msg[:, :].rearrange("p (g f) -> p g f", f=FD)
        hot3 = hot[:, :].rearrange("p (g n) -> p g n", n=P)
        stats2 = stats[:, :, :].rearrange("p n s -> p (n s)")

        s_raw = sem("s_raw")
        s_x = sem("s_x")
        s_w = sem("s_w")
        s_wz = sem("s_wz")
        s_xz = sem("s_xz")
        s_iota = sem("s_iota")
        s_const = sem("s_const")
        s_constf = sem("s_constf")
        s_flt = sem("s_flt")
        s_span = sem("s_span")
        s_spand = sem("s_spand")
        s_xb = sem("s_xb")
        s_tab = sem("s_tab")
        s_zero = sem("s_zero")
        idx_turned = sem("idx_turned")
        idx_taken = sem("idx_taken")
        held = sem("held")
        gathered = [sem(f"gathered{s}") for s in range(RING)]
        rows_free = sem("rows_free")
        ea_in = [sem(f"ea_in{s}") for s in range(RING)]
        ea_turned = sem("ea_turned")
        eaT_taken = sem("eaT_taken")
        embedded = sem("embedded")
        relu_done = sem("relu_done")
        hot_ready = sem("hot_ready")
        seg_done = sem("seg_done")
        acc_done = sem("acc_done")
        m_h = sem("m_h")
        m_T = sem("m_T")
        m_Tc = sem("m_Tc")
        m_1 = sem("m_1")
        m_1a = sem("m_1a")
        m_2 = sem("m_2")
        m_2a = sem("m_2a")
        m_st = sem("m_st")
        s_bn = sem("s_bn")
        s_bna = sem("s_bna")
        s_deg = sem("s_deg")
        s_dega = sem("s_dega")
        b_a = sem("b_a")
        b_T = sem("b_T")
        b_y = sem("b_y")
        ln = sem("ln")
        ln_v = sem("ln_v")
        ln_r = sem("ln_r")
        s_g = sem("s_g")
        s_res = sem("s_res")
        s_out = sem("s_out")

        block = ctx.enter_context(nc.Block())

        def hold(eng, semaphore, value):
            eng.wait_ge(semaphore, value)
            eng.sem_inc(held, 1)

        def nodes(t):
            return t.rearrange("(w p) f -> p w f", p=P)

        @block.sync
        def _(sp):
            for n, t in (("src", src), ("dst", dst)):
                sp.dma_start(raw[n], t.rearrange("(r e) -> r e", r=ROWS)).then_inc(s_raw, 16)
            sp.wait_ge(s_xz, 1)
            sp.dma_start(xs3[:, 0:WINDOWS - 1, :], nodes(x[0:N - TAIL, :])).then_inc(s_x, 16)
            sp.dma_start(xs3[0:TAIL, WINDOWS - 1, :], x[N - TAIL:N, :]).then_inc(s_x, 16)
            sp.dma_start(be_all[:, :], be.rearrange("(a f) -> a f", a=1).to_broadcast([P, F])).then_inc(s_x, 16)
            sp.wait_ge(s_wz, 1)
            for j in range(4):
                sp.dma_start(We4[j * D:(j + 1) * D, j * F:(j + 1) * F], We).then_inc(s_w, 16)
            sp.dma_start(W1_sb[:, :], W1).then_inc(s_w, 16)
            sp.dma_start(W2_sb[:, :], W2).then_inc(s_w, 16)
            for j, t in enumerate((b1, b2, gamma, beta)):
                sp.dma_start(cols[:, j:j + 1], t.rearrange("(f a) -> f a", a=1)).then_inc(s_w, 16)
            sp.wait_ge(s_span, 5)
            sp.dma_start(span_dram.rearrange("(r s) -> r s", r=ROWS),
                         span_w[:, :, :].rearrange("r k s -> r (k s)")).then_inc(s_spand, 16)
            sp.wait_ge(s_spand, 16)
            sp.dma_start(span[:, :], span_dram.rearrange("(a s) -> a s", a=1)).then_inc(s_spand, 16)
            sp.wait_ge(s_xb, 1)
            sp.dma_start(nodes(xb_dram), agg3[:, :, 0:F]).then_inc(s_tab, 16)
            ea_v = ea.rearrange("(k p g) d -> k p (g d)", p=P, g=G)
            with sp.Fori(0, TURNS) as t:
                for s in range(RING):
                    sp.wait_ge(ea_turned, t * RING + s + 1)
                    sp.dma_start(ea_sb[:, s, :], ea_v[bass.ds(t * RING + s, 1), :, :].rearrange("k p e -> (k p) e")
                                 ).then_inc(ea_in[s], 16)
            for h in range(2):
                sp.wait_ge(s_g, h + 1)
                sp.dma_start(nodes(g_dram[h]), agg3[:, :, 0:F]).then_inc(s_tab, 16)
            sp.wait_ge(s_res, GROUPS)
            sp.dma_start(nodes(out[0:N - TAIL, :]), xs3[:, 0:WINDOWS - 1, :]).then_inc(s_out, 16)
            sp.dma_start(out[N - TAIL:N, :], xs3[0:TAIL, WINDOWS - 1, :]).then_inc(s_out, 16)
            sp.wait_ge(s_out, 32)

        @block.gpsimd
        def _(pool):
            nc.gpsimd.memset(xs3[:, WINDOWS - 1, :], 0.0).then_inc(s_xz, 1)
            nc.gpsimd.memset(We4[:, :], 0.0).then_inc(s_wz, 1)
            nc.gpsimd.memset(ident[:, :], 0.0).then_inc(s_iota, 1)
            nc.gpsimd.memset(eps[:, :], EPS).then_inc(s_const, 1)
            nc.gpsimd.iota(node_i[:, :], pattern=[[1, P]], base=0, channel_multiplier=0).then_inc(s_const, 1)
            nc.gpsimd.iota(base_i[:, :], pattern=[[P, WINDOWS]], base=0, channel_multiplier=0).then_inc(s_const, 1)
            pool.wait_ge(s_iota, 1)
            nc.gpsimd.affine_select(out=ident[:, :], in_=ident[:, :], compare_op=ALU.not_equal, fill=1.0, base=0,
                                    pattern=[[-1, P]], channel_multiplier=1).then_inc(s_const, 1)
            pool.wait_ge(idx_taken, 2 * RING * G + 2)
            for p in range(3):
                table = [xb_dram, *g_dram][p]
                pool.wait_ge(s_tab, 16 * (p + 1))
                with pool.Fori(0, TURNS) as t:
                    for s in range(RING):
                        hold(pool, rows_free, t * RING + (p * SUPERS + s + 1))
                        for g in range(G):
                            pool.indirect_dma_start(
                                rows[:, s, g * F:(g + 1) * F], None, table,
                                bass.IndirectOffsetOnAxis(ap=idx[:, s * G + g:s * G + g + 1], axis=0),
                            ).then_inc(gathered[s], 16)

        def visits(eng, t, s):
            lo = eng.value_load(span[0:1, bass.ds(t * (2 * RING) + 2 * s, 1)], min_val=0, max_val=WINDOWS - 1)
            hi = eng.value_load(span[0:1, bass.ds(t * (2 * RING) + (2 * s + 1), 1)], min_val=0, max_val=WINDOWS - 1)
            return lo, hi + 1

        @block.tensor
        def _(pe):
            pe.wait_ge(s_const, 4)
            pe.wait_ge(s_flt, 2)
            for b in range(RING):
                for g in range(G):
                    if b:
                        pe.wait_ge(idx_taken, 2 * ((b - 1) * G + g + 1))
                    for i, n in enumerate(("src", "dst")):
                        v = flt[n][:, b * SUPER:(b + 1) * SUPER].rearrange("r (q g) -> r g q", g=G)[:, g, :]
                        nc.tensor.transpose(bank[g][:, i * P:i * P + ROWS], v, ident[0:ROWS, 0:ROWS]).then_inc(idx_turned, 1)

            seen = pe.alloc_register()
            pe.reg_mov(seen, 0)

            def segment(t, s, rhs, width):
                lo, hi = visits(pe, t, s)
                with pe.Fori(lo, hi):
                    n = pe.snap(seen)
                    pe.wait_ge(hot_ready, n + 1)
                    pe.wait_ge(acc_done, n + 1)
                    for g in range(G):
                        mm = nc.tensor.matmul(seg_ps[:, 0:width], hot3[:, g, :], rhs(g), start=(g == 0), stop=(g == G - 1))
                    mm.then_inc(seg_done, 1)
                    pe.reg_add(seen, seen, 1)

            def embed(t, s):
                k = t * RING + s
                pe.wait_ge(ea_in[s], t * 16 + 16)
                pe.wait_ge(eaT_taken, k + 1)
                nc.tensor.transpose(eaT_ps[:, 0:P], ea_sb[:, s, 0:P], ident[:, :])
                nc.tensor.transpose(eaT_ps[0:D, P:2 * P], ea_sb[:, s, P:P + D], ident[:, :]).then_inc(ea_turned, 1)
                pe.wait_ge(eaT_taken, k + 2)
                pe.wait_ge(rows_free, k + (RING if s == 0 else RING - 1))
                nc.tensor.matmul(emb_ps[s % 2][:, 0:4 * F], eaT[:, 0:P], We4[:, :], start=True, stop=True)
                nc.tensor.matmul(emb_ps[s % 2][:, 4 * F:5 * F], eaT[0:D, P:2 * P], We4[0:D, 0:F],
                                 start=True, stop=True).then_inc(embedded, 1)

            pe.wait_ge(s_w, 160)
            pe.wait_ge(s_spand, 32)
            pe.wait_ge(idx_taken, 2 * RING * G)
            embed(0, 0)

            def turn(t, last):
                for s in range(RING):
                    if s < RING - 1:
                        embed(t, s + 1)
                    elif not last:
                        embed(t + 1, 0)
                    pe.wait_ge(relu_done, t * RING + s + 1)
                    segment(t, s, lambda g: msg3[:, g, :], FD)

            with pe.Fori(0, TURNS - 1) as t:
                turn(t, False)
            turn(TURNS - 1, True)

            def mlp(j, nw):
                c = nw * P
                pe.wait_ge(m_h, j + 1)
                pe.wait_ge(m_Tc, j + 1)
                for i in range(nw):
                    tr = nc.tensor.transpose(bank[4][0:F, i * P:(i + 1) * P], hs[:, i, :], ident[:, :])
                tr.then_inc(m_T, 1)
                pe.wait_ge(m_Tc, j + 2)
                pe.wait_ge(m_1a, j + 1)
                nc.tensor.matmul(bank[5][0:F, 0:c], W1_sb[:, :], hT[:, 0:c], start=True, stop=True).then_inc(m_1, 1)
                pe.wait_ge(m_1a, j + 2)
                pe.wait_ge(m_2a, j + 1)
                nc.tensor.matmul(bank[6][0:F, 0:c], W2_sb[:, :], hid[:, 0:c], start=True, stop=True).then_inc(m_2, 1)

            with pe.Fori(0, GROUPS - 1) as j:
                mlp(j, GROUP)
            mlp(GROUPS - 1, LAST)

            def back(j, nw):
                pe.wait_ge(b_a, j + 1)
                pe.wait_ge(b_y, j + 1)
                for i in range(nw):
                    tr = nc.tensor.transpose(bank[4][:, i * F:(i + 1) * F], yT[:, i * P:(i + 1) * P], ident[0:F, 0:F])
                tr.then_inc(b_T, 1)

            with pe.Fori(0, GROUPS - 1) as j:
                back(j, GROUP)
            back(GROUPS - 1, LAST)

            for h in range(2):
                with pe.Fori(0, TURNS) as t:
                    for s in range(RING):
                        pe.wait_ge(gathered[s], t * (16 * G) + 16 * G * ((h + 1) * TURNS + 1))
                        segment(t, s, lambda g: rows[:, s, g * F:(g + 1) * F], F)

        @block.scalar
        def _(act):
            def take(t, s):
                k = t * RING + s
                act.wait_ge(embedded, k + 1)
                act.wait_ge(ea_turned, k + RING + 1)
                nc.scalar.copy(eaT[:, 0:P], eaT_ps[:, 0:P])
                nc.scalar.copy(eaT[0:D, P:2 * P], eaT_ps[0:D, P:2 * P]).then_inc(eaT_taken, 1)

            act.sem_inc(eaT_taken, 1)
            act.sem_inc(m_1a, 1)
            act.sem_inc(m_2a, 1)
            take(0, 0)

            def turn(t, last):
                for s in range(RING):
                    if s < RING - 1:
                        take(t, s + 1)
                    elif not last:
                        take(t + 1, 0)
                    act.wait_ge(rows_free, t * RING + (RING + s + 1))
                    nc.scalar.activation(msg3[:, :, 0:F], msg3[:, :, 0:F], ACT.Relu).then_inc(relu_done, 1)

            with act.Fori(0, TURNS - 1) as t:
                turn(t, False)
            turn(TURNS - 1, True)

            act.wait_ge(s_deg, 1)
            nc.scalar.activation(root[:, :], deg[:, :], ACT.Sqrt).then_inc(s_dega, 1)

            def mlp(j, nw):
                c = nw * P
                act.wait_ge(m_1, j + 2)
                act.wait_ge(m_2, j + 1)
                nc.scalar.activation(hid[:, 0:c], bank[5][0:F, 0:c], ACT.Relu, bias=cols[:, 0:1]).then_inc(m_1a, 1)
                act.wait_ge(m_2, j + 2)
                nc.scalar.activation(h2T[:, bass.ds(j * GN, c)], bank[6][0:F, 0:c], ACT.Identity, bias=cols[:, 1:2]).then_inc(m_2a, 1)

            act.sem_inc(m_2, 1)
            act.wait_ge(s_w, 160)
            with act.Fori(0, GROUPS - 1) as j:
                mlp(j, GROUP)
            mlp(GROUPS - 1, LAST)

            act.wait_ge(s_bn, 1)
            nc.scalar.activation(bn[:, 0:1], mv[:, 1:2], ACT.Sqrt, bias=eps[0:F, :]).then_inc(s_bna, 1)
            act.sem_inc(b_T, 1)
            act.wait_ge(s_bn, 5)

            def scale(j, nw):
                c = nw * P
                act.wait_ge(b_T, j + 1)
                nc.scalar.activation(yT[:, 0:c], h2T[:, bass.ds(j * GN, c)], ACT.Relu, bias=bn[:, 3:4], scale=bn[:, 2:3]).then_inc(b_a, 1)

            def ln_root(n):
                act.wait_ge(ln_v, n + 1)
                nc.scalar.activation(lroot[:, :], lmv[:, :, 1], ACT.Sqrt, bias=eps[:, :]).then_inc(ln_r, 1)

            with act.Fori(0, GROUPS - 1) as j:
                scale(j, GROUP)
                ln_root(j)
            scale(GROUPS - 1, LAST)
            ln_root(GROUPS - 1)
            with act.Fori(0, GROUPS) as j:
                ln_root(j + GROUPS)

        @block.vector
        def _(dve):
            dve.sem_inc(rows_free, RING)
            dve.sem_inc(ea_turned, RING)
            dve.sem_inc(embedded, 1)
            dve.sem_inc(acc_done, 1)
            dve.sem_inc(m_Tc, 1)
            dve.sem_inc(b_y, 1)
            nc.vector.memset(msg3[:, :, F:FD], 1.0).then_inc(s_constf, 1)
            nc.vector.memset(lmv[:, :, :], 1.0).then_inc(s_constf, 1)
            dve.wait_ge(s_raw, 32)
            for n in ("dst", "src"):
                nc.vector.tensor_copy(flt[n], raw[n]).then_inc(s_flt, 1)
            dve.wait_ge(s_flt, 1)
            d3 = flt["dst"].rearrange("r (k e) -> r k e", e=SUPER)
            nc.vector.tensor_reduce(span_f[:, :, 0], d3, AX_X, ALU.min).then_inc(s_span, 1)
            nc.vector.tensor_reduce(span_f[:, :, 1], d3, AX_X, ALU.max).then_inc(s_span, 1)
            dve.wait_ge(s_span, 2)
            nc.vector.tensor_scalar(span_f[:, :, :], span_f[:, :, :], float(N - 1), None, ALU.min).then_inc(s_span, 1)
            dve.wait_ge(s_span, 3)
            nc.vector.tensor_copy(span_n[:, :, :], span_f[:, :, :]).then_inc(s_span, 1)
            dve.wait_ge(s_span, 4)
            nc.vector.tensor_scalar(span_w[:, :, :], span_n[:, :, :], 7, None, ALU.arith_shift_right).then_inc(s_span, 1)
            dve.wait_ge(s_x, 48)
            nc.vector.tensor_tensor(agg3[:, :, 0:F], xs3, be_all[:, :].unsqueeze(1).to_broadcast([P, WINDOWS, F]),
                                    ALU.add).then_inc(s_xb, 1)
            dve.wait_ge(s_const, 4)
            nc.vector.tensor_copy(node[:, :], node_i[:, :]).then_inc(s_constf, 1)
            nc.vector.tensor_copy(base[:, :], base_i[:, :]).then_inc(s_constf, 1)
            srcv = src_all[:, 0:SUPERS * G].rearrange("q (r c) -> q c r", c=RING * G)
            dstv = dst_all[:, :].rearrange("q (r c) -> q c r", c=RING * G)
            for b in range(RING):
                for g in range(G):
                    for i, v in enumerate((srcv, dstv)):
                        dve.wait_ge(idx_turned, 2 * (b * G + g + 1))
                        nc.vector.tensor_copy(v[:, b * G + g, :],
                                              bank[g][:, i * P:i * P + ROWS]).then_inc(idx_taken, 1)
            dve.wait_ge(idx_taken, 2 * RING * G)
            for to in (idx[:, :], src_all[:, SUPERS * G:]):
                nc.vector.tensor_copy(to, src_all[:, 0:RING * G]).then_inc(idx_taken, 1)
            dve.wait_ge(s_tab, 16)
            nc.vector.memset(agg[:, :], 0.0).then_inc(s_zero, 1)
            dve.wait_ge(s_spand, 32)
            dve.wait_ge(s_constf, 4)
            dve.wait_ge(s_zero, 1)
            dve.wait_ge(idx_taken, 2 * RING * G + 2)

            def stage(t, s):
                nc.vector.tensor_copy(idx[:, s * G:(s + 1) * G], src_all[:, bass.ds(t * (RING * G) + (RING + s) * G, G)])

            seen = dve.alloc_register()
            dve.reg_mov(seen, 0)

            def accumulate(t, s, width):
                lo, hi = visits(dve, t, s)
                d = dst_all[:, bass.ds(t * (RING * G) + s * G, G)].unsqueeze(2).to_broadcast([P, G, P])
                with dve.Fori(lo, hi) as w:
                    n = dve.snap(seen)
                    nc.vector.scalar_tensor_tensor(out=hot3, in0=d, scalar=base[:, bass.ds(w, 1)],
                                                   in1=node[:, :].unsqueeze(1).to_broadcast([P, G, P]),
                                                   op0=ALU.subtract, op1=ALU.is_equal).then_inc(hot_ready, 1)
                    dve.wait_ge(seg_done, n + 1)
                    dve.wait_ge(acc_done, n + 1)
                    a = agg[:, bass.ds(w * FD, width)]
                    nc.vector.tensor_tensor(a, a, seg_ps[:, 0:width], ALU.add).then_inc(acc_done, 1)
                    dve.reg_add(seen, seen, 1)

            with dve.Fori(0, TURNS) as t:
                for s in range(RING):
                    dve.wait_ge(gathered[s], t * (16 * G) + 16 * G)
                    stage(t, s)
                    dve.wait_ge(embedded, t * RING + (s + 2))
                    nc.vector.tensor_tensor(msg3[:, :, 0:F], rows[:, s, :].rearrange("p (g f) -> p g f", f=F),
                                            emb_ps[s % 2][:, 0:G * F].rearrange("p (g f) -> p g f", f=F),
                                            ALU.add).then_inc(rows_free, 1)
                    accumulate(t, s, FD)

            n = dve.snap(seen)
            hold(dve, acc_done, n + 1)
            nc.vector.tensor_scalar(deg[:, :], agg3[:, :, F], 1.0, None, ALU.add).then_inc(s_deg, 1)
            dve.wait_ge(s_deg, 1)
            nc.vector.reciprocal(inv[:, :], deg[:, :]).then_inc(s_deg, 1)
            dve.wait_ge(s_dega, 1)
            nc.vector.reciprocal(dis[:, :], root[:, :]).then_inc(s_deg, 1)

            def mlp(j, nw):
                c = nw * P
                dve.wait_ge(m_T, j + 1)
                nc.vector.tensor_tensor(hs[:, 0:nw, :],
                                        agg[:, bass.ds(j * (GROUP * FD), nw * FD)].rearrange("p (w f) -> p w f", f=FD)[:, :, 0:F],
                                        xs[:, bass.ds(j * (GROUP * F), nw * F)].rearrange("p (w f) -> p w f", f=F),
                                        ALU.add).then_inc(m_h, 1)
                dve.wait_ge(m_T, j + 2)
                dve.wait_ge(m_1, j + 1)
                nc.vector.tensor_copy(hT[:, 0:c], bank[4][0:F, 0:c]).then_inc(m_Tc, 1)

            dve.sem_inc(m_1, 1)
            dve.sem_inc(m_T, 1)
            with dve.Fori(0, GROUPS - 1) as j:
                mlp(j, GROUP)
            mlp(GROUPS - 1, LAST)
            for c in range(N // BN):
                dve.wait_ge(m_2a, 1 + min(GROUPS, -(-(c + 1) * BN // GN)))
                nc.vector.bn_stats(stats[:, c, :], h2T[:, c * BN:(c + 1) * BN]).then_inc(m_st, 1)
            dve.wait_ge(m_st, N // BN)
            nc.vector.bn_aggr(mv[:, :], stats2).then_inc(s_bn, 1)
            dve.wait_ge(s_bna, 1)
            nc.vector.reciprocal(bn[:, 1:2], bn[:, 0:1]).then_inc(s_bn, 1)
            dve.wait_ge(s_bn, 2)
            nc.vector.tensor_tensor(bn[:, 2:3], bn[:, 1:2], cols[:, 2:3], ALU.mult).then_inc(s_bn, 1)
            dve.wait_ge(s_bn, 3)
            nc.vector.tensor_tensor(bnt[:, :], mv[:, 0:1], bn[:, 2:3], ALU.mult).then_inc(s_bn, 1)
            dve.wait_ge(s_bn, 4)
            nc.vector.tensor_tensor(bn[:, 3:4], cols[:, 3:4], bnt[:, :], ALU.subtract).then_inc(s_bn, 1)

            CH = 5

            def layer_norm(j, nw, m, done):
                w0 = j * GROUP
                xw = [xs[:, bass.ds((w0 + i) * F, F)] for i in range(nw)]
                hold(dve, ln, m * CH + 1)
                for i in range(nw):
                    st = nc.vector.bn_stats(lst[:, i, :], xw[i])
                st.then_inc(ln, 1)
                hold(dve, ln, m * CH + 2)
                for i in range(nw):
                    ag = nc.vector.bn_aggr(lmv[:, i, :], lst[:, i, :])
                ag.then_inc(ln_v, 1)
                dve.wait_ge(ln_r, m + 1)
                nc.vector.reciprocal(lrs[:, :], lroot[:, :]).then_inc(ln, 1)
                dve.wait_ge(ln, m * CH + 3)
                for i in range(nw):
                    ts = nc.vector.tensor_scalar(xw[i], xw[i], lmv[:, i, 0:1], lrs[:, i:i + 1], ALU.subtract, ALU.mult)
                ts.then_inc(ln, 1)
                if done is not None:
                    dve.wait_ge(ln, m * CH + 4)

            def first_norm(j, nw):
                w0 = j * GROUP
                xw = xs[:, bass.ds(w0 * F, nw * F)]
                dve.wait_ge(b_T, j + 2)
                nc.vector.tensor_tensor(xw, xw, bank[4][:, 0:nw * F], ALU.add).then_inc(b_y, 1)
                hold(dve, b_y, j + 2)
                layer_norm(j, nw, j, True)
                av = agg[:, bass.ds(w0 * FD, nw * FD)].rearrange("p (w f) -> p w f", f=FD)[:, :, 0:F]
                nc.vector.tensor_tensor(av, xw.rearrange("p (w f) -> p w f", f=F),
                                        dis[:, bass.ds(w0, nw)].unsqueeze(2).to_broadcast([P, nw, F]),
                                        ALU.mult).then_inc(ln, 2)

            dve.sem_inc(ln, 1)
            dve.wait_ge(s_deg, 3)
            with dve.Fori(0, GROUPS - 1) as j:
                first_norm(j, GROUP)
            first_norm(GROUPS - 1, LAST)
            dve.wait_ge(ln, GROUPS * CH + 1)
            dve.sem_inc(s_g, 1)

            for h in range(2):
                dve.wait_ge(s_tab, 16 * (h + 2))
                with dve.Fori(0, TURNS) as t:
                    for s in range(RING):
                        dve.wait_ge(gathered[s], t * (16 * G) + 16 * G * ((h + 1) * TURNS + 1))
                        stage(t, s)
                        accumulate(t, s, F)
                        dve.sem_inc(rows_free, 1)
                n = dve.snap(seen)
                hold(dve, acc_done, n + 1)
                if h == 0:
                    nc.vector.tensor_tensor(agg3[:, :, 0:F], agg3[:, :, 0:F],
                                            inv[:, :].unsqueeze(2).to_broadcast([P, WINDOWS, F]),
                                            ALU.mult).then_inc(s_g, 1)
                    dve.wait_ge(s_g, 2)

            def second_norm(j, nw):
                w0 = j * GROUP
                for i in range(nw):
                    xw = xs[:, bass.ds((w0 + i) * F, F)]
                    st = nc.vector.scalar_tensor_tensor(out=xw, in0=agg[:, bass.ds((w0 + i) * FD, F)],
                                                        scalar=dis[:, bass.ds(w0 + i, 1)], in1=xw,
                                                        op0=ALU.mult, op1=ALU.add)
                st.then_inc(b_y, 1)
                hold(dve, b_y, j + (GROUPS + 2))
                layer_norm(j, nw, j + GROUPS, True)
                dve.sem_inc(ln, 2)
                dve.sem_inc(s_res, 1)

            with dve.Fori(0, GROUPS - 1) as j:
                second_norm(j, GROUP)
            second_norm(GROUPS - 1, LAST)


_INS = ['x', 'src', 'dst', 'edge_attr_32', 'L0_gnn_We', 'L0_gnn_be', 'L0_gnn_W1', 'L0_gnn_b1',
        'L0_gnn_W2', 'L0_gnn_b2', 'L0_gnn_gamma', 'L0_gnn_beta']
_OUTS = [((12500, 96), 'float32')]


def kernel(**inputs):
    import numpy as _np
    import concourse.bacc as _bacc
    from concourse import mybir as _mybir
    from concourse.bass_utils import run_bass_kernel_spmd as _run

    nc = _bacc.Bacc("TRN2", target_bir_lowering=False, num_devices=1)
    arrays, args = {}, []
    for name in _INS:
        a = _np.ascontiguousarray(inputs[name])
        arrays[f"in_{name}_dram"] = a
        args.append(nc.dram_tensor(f"in_{name}_dram", a.shape, _mybir.dt.from_np(a.dtype), kind="ExternalInput").ap())
    for i, (shape, dtype) in enumerate(_OUTS):
        dt = _mybir.dt.from_np(_np.dtype(dtype))
        args.append(nc.dram_tensor(f"out_{i}_dram", shape, dt, kind="ExternalOutput").ap())
    gnn_kernel(nc, *args)
    r = _run(nc, [arrays], core_ids=[0])
    return r.results[0]["out_0_dram"]
```

```python
from contextlib import ExitStack

import concourse.bass as bass
from concourse import mybir

F32 = mybir.dt.float32
I32 = mybir.dt.int32
U32 = mybir.dt.uint32
BF16 = mybir.dt.bfloat16
F16 = mybir.dt.float16
ALU = mybir.AluOpType
ACT = mybir.ActivationFunctionType
AX_X = mybir.AxisListType.X

P = 128
EPS = 1e-5


def gnn_kernel(nc, x, src, dst, ea, We, be, W1, b1, W2, b2, gamma, beta, out):
    N, F = x.shape
    E, D = ea.shape
    WINDOWS = -(-N // P)
    TAIL = N - (WINDOWS - 1) * P
    G = 5
    SUPER = G * P
    SUPERS = E // SUPER
    RING = 5
    TURNS = SUPERS // RING
    SLOT = (0, 1, 0, 1, 2)
    ROWS = SUPERS // RING
    assert E % (SUPER * RING) == 0 and ROWS <= P and 4 * D == P and F * G <= 512
    FD = F + 1
    GROUP = 4
    GROUPS = -(-WINDOWS // GROUP)
    GN = GROUP * P
    LAST = WINDOWS - (GROUPS - 1) * GROUP
    BN = 500
    assert N % BN == 0 and GROUPS % 2 == 1

    DENSE = 24
    SUBN = 4
    SUBS = DENSE * P // SUBN
    SUBW = WINDOWS * SUBN
    HALF = SUBW // 2
    PER = 2
    TV = PER * RING
    VISITS = PER * SUPERS
    CHUNKS = E // P
    PAIRS = -(-CHUNKS // 2)
    CG = -(-(SUBS + 1) // P)
    HOTS = 3 * PER
    DIV = 1024
    assert SUBW <= 512 and WINDOWS % 2 == 0 and VISITS <= PAIRS and SUBS + TV <= DIV
    a_dram = nc.dram_tensor("counts_scratch", (P, 2, SUBS + TV, HALF), F32, kind="Internal").ap()
    cnt_dram = nc.dram_tensor("pairs_scratch", (CG * P,), F32, kind="Internal").ap()
    x1_dram = nc.dram_tensor("x1_scratch", (WINDOWS * P, F), F32, kind="Internal").ap()
    xb_dram = nc.dram_tensor("xb_scratch", (WINDOWS * P, F), F32, kind="Internal").ap()
    g_dram = [nc.dram_tensor(f"g{h}_scratch", (WINDOWS * P, F), F32, kind="Internal").ap() for h in range(2)]
    SPAN = 2 * RING + 2
    assert SPAN % 4 == 0
    span_dram = nc.dram_tensor("span_scratch", (TURNS, SPAN), I32, kind="Internal").ap()

    with ExitStack() as ctx:
        def sb(name, shape, dt=F32):
            return ctx.enter_context(nc.sbuf_tensor(name, shape, dt))

        def sem(name):
            return ctx.enter_context(nc.semaphore(name))

        bank = [ctx.enter_context(nc.psum_tensor(f"bank{i}", [P, 512], F32)) for i in range(5)]
        count_ps = ctx.enter_context(nc.psum_tensor("count_ps", [P, 3 * 512], F32))
        bank += [count_ps[:, i * 512:(i + 1) * 512] for i in range(3)]
        eaT_ps = bank[0]
        seg_ps = [bank[3], bank[4]]
        emb_ps = [bank[1], bank[2]]

        ident = sb("ident", [P, P])
        node_i = sb("node_i", [P, P], I32)
        node = sb("node", [P, P])
        base_i = sb("base_i", [P, WINDOWS], I32)
        base = sb("base", [P, WINDOWS])
        sub_base = sb("sub_base", [P, SUBS])
        key_i = sb("key_i", [P, SUBW], I32)
        zero_b = sb("zero_b", [P, P], BF16)
        pick = sb("pick", [P, P])
        ones = sb("ones", [P, P])
        thr_i = sb("thr_i", [P, CG], I32)
        thr = sb("thr", [P, CG])
        cnt_f = sb("cnt_f", [P, CG])
        cnt_g = sb("cnt_g", [P, CG])
        vis_i = sb("vis_i", [ROWS, TV + 2], I32)
        vis = sb("vis", [ROWS, TV + 2])
        spare_i = sb("spare_i", [ROWS, TV], I32)
        spare = sb("spare", [ROWS, TV])
        sub = sb("sub", [ROWS, TV + 2])
        sub_n = sb("sub_n", [ROWS, TV], I32)
        par_n = sb("par_n", [ROWS, TV], I32)
        fields = sb("fields", [ROWS, 8, TV])
        packed = sb("packed", [ROWS, 4, RING, 2])
        tab_dve = sb("tab_dve", [ROWS, 12], I32)
        tab_pe = sb("tab_pe", [ROWS, 8], I32)
        tab_act = sb("tab_act", [ROWS, 8], I32)
        nxt_i = sb("nxt_i", [ROWS, 1], I32)
        nxt = sb("nxt", [ROWS, 1])
        checks = sb("checks", [ROWS, 4])
        check2 = sb("check2", [ROWS, 2])
        dense_f = sb("dense_f", [P, 2])
        lim = sb("lim", [P, 1])
        total = sb("total", [P, 2])
        okay = sb("okay", [P, 1])
        ctl_f = sb("ctl_f", [1, 8])
        ctl = sb("ctl", [1, 4], I32)
        eps = sb("eps", [P, 1])
        wide = sb("wide", [P, 4 * RING * SUPER])
        raw = {n: wide[0:ROWS, i * RING * SUPER:(i + 1) * RING * SUPER].bitcast(I32) for i, n in enumerate(("src", "dst"))}
        flt = {n: wide[0:ROWS, (2 + i) * RING * SUPER:(3 + i) * RING * SUPER] for i, n in enumerate(("src", "dst"))}
        h2T = wide[0:F, 0:WINDOWS * P]
        C2 = 2 * PAIRS
        src_c, dst_c = (wide[:, i * C2:(i + 1) * C2] for i in range(2))
        src_ci, dst_ci = src_c.bitcast(I32), dst_c.bitcast(I32)
        at = 2 * RING * SUPER
        stage_a = wide[:, at:at + 3 * PER * SUBW].rearrange("p (s h c) -> p s h c", s=HOTS, h=2)
        at += 3 * PER * SUBW
        key_hot = wide[:, at:at + HOTS * SUBW].bitcast(BF16)
        at += HOTS * SUBW
        low_hot = wide[:, at:at + HOTS * P].bitcast(BF16)
        at += HOTS * P
        key_no = wide[:, at:at + SUBW // 2].bitcast(F16)
        assert at + SUBW // 2 <= 4 * RING * SUPER and 2 * C2 <= 2 * RING * SUPER
        blocks = [wide[:, h * (P // SUBN) * HALF:(h + 1) * (P // SUBN) * HALF].rearrange("p (n v) -> p n v", v=WINDOWS // 2) for h in range(2)]
        assert 2 * (P // SUBN) * HALF <= 4 * RING * SUPER
        src_all = sb("src_all", [P, SUPERS * G], U32)
        dst_all = sb("dst_all", [P, SUPERS * G])
        span_f = sb("span_f", [ROWS, RING, 2])
        span_n = sb("span_n", [ROWS, RING, 2], I32)
        span_w = sb("span_w", [ROWS, RING, 2], I32)
        span = sb("span", [1, TURNS * SPAN], I32)
        xs = sb("xs", [P, WINDOWS * F])
        agg = sb("agg", [P, WINDOWS * FD])
        dis = sb("dis", [P, WINDOWS])
        inv = sb("inv", [P, WINDOWS])
        deg = sb("deg", [P, WINDOWS])
        root = sb("root", [P, WINDOWS])
        be_all = sb("be_all", [P, F])
        We4 = sb("We4", [P, 4 * F])
        W1_sb = sb("W1_sb", [F, F])
        W2_sb = sb("W2_sb", [F, F])
        cols = sb("cols", [F, 4])
        idx = sb("idx", [P, RING * G], U32)
        rows = sb("rows", [P, RING, G * F])
        ea_sb = sb("ea_sb", [P, RING, G * D])
        eaT = sb("eaT", [P, 2 * P])
        msg = sb("msg", [P, 3, G * FD])
        hot = sb("hot", [P, 6, SUPER])
        flat = msg[:, :, :].rearrange("p s e -> p (s e)")
        hs = flat[:, 0:GROUP * F].rearrange("p (w f) -> p w f", f=F)
        hT, hid = (flat[0:F, GROUP * F + i * GN:GROUP * F + (i + 1) * GN] for i in range(2))
        yT = hT
        sub_i = ea_sb[:, :, :].rearrange("p s e -> p (s e)")[:, 0:SUBS].bitcast(I32)
        stats = sb("stats", [F, N // BN, 6])
        mv = sb("mv", [F, 2])
        bn = sb("bn", [F, 4])
        bnt = sb("bnt", [F, 1])
        lst = sb("lst", [P, GROUP, 6])
        lmv = sb("lmv", [P, GROUP, 2])
        lroot = sb("lroot", [P, GROUP])
        lrs = sb("lrs", [P, GROUP])

        agg3 = agg[:, :].rearrange("p (w f) -> p w f", f=FD)
        xs3 = xs[:, :].rearrange("p (w f) -> p w f", f=F)
        msg3 = [msg[:, s, :].rearrange("p (g f) -> p g f", f=FD) for s in SLOT]
        hot3, second3 = ([hot[:, i + s, :].rearrange("p (g n) -> p g n", n=P) for s in SLOT] for i in (0, 3))
        last_dst = hot[:, :, :].rearrange("p s e -> p (s e)")
        CNT_AT, END_AT = 6144, 7168
        stats2 = stats[:, :, :].rearrange("p n s -> p (n s)")

        s_raw = sem("s_raw")
        s_x = sem("s_x")
        s_w = sem("s_w")
        s_wz = sem("s_wz")
        s_xz = sem("s_xz")
        s_iota = sem("s_iota")
        s_const = sem("s_const")
        s_constf = sem("s_constf")
        s_flt = sem("s_flt")
        s_span = sem("s_span")
        s_spand = sem("s_spand")
        s_xb = sem("s_xb")
        s_tab = sem("s_tab")
        s_zero = sem("s_zero")
        s_cut = sem("s_cut")
        s_key = sem("s_key")
        s_nxt = sem("s_nxt")
        s_chk = sem("s_chk")
        s_tot = sem("s_tot")
        s_ctl = sem("s_ctl")
        s_ctlf = sem("s_ctlf")
        s_cnt = sem("s_cnt")
        s_cntp = sem("s_cntp")
        s_cntd = sem("s_cntd")
        flat_turned = sem("flat_turned")
        flat_taken = sem("flat_taken")
        pair_hot = sem("pair_hot")
        s_vis = sem("s_vis")
        s_low = sem("s_low")
        visit_done = sem("visit_done")
        visit_copied = sem("visit_copied")
        stored = [sem(f"stored{i}") for i in range(HOTS)]
        block_in = [sem(f"block_in{h}") for h in range(2)]
        block_used = [sem(f"block_used{h}") for h in range(2)]
        dense_done = sem("dense_done")
        dense_acc = sem("dense_acc")
        s_x1 = sem("s_x1")
        s_gc = sem("s_gc")
        idx_turned = sem("idx_turned")
        idx_taken = sem("idx_taken")
        held = sem("held")
        gathered = [sem(f"gathered{s}") for s in range(RING)]
        rows_free = sem("rows_free")
        ea_in = [sem(f"ea_in{s}") for s in range(RING)]
        ea_turned = sem("ea_turned")
        eaT_taken = sem("eaT_taken")
        embedded = sem("embedded")
        relu_done = sem("relu_done")
        hot_ready = sem("hot_ready")
        seg_done = sem("seg_done")
        acc_done = sem("acc_done")
        second_hot = sem("second_hot")
        second_seg = sem("second_seg")
        more_hot = sem("more_hot")
        more_seg = sem("more_seg")
        more_acc = sem("more_acc")
        m_h = sem("m_h")
        m_T = sem("m_T")
        m_Tc = sem("m_Tc")
        m_1 = sem("m_1")
        m_1a = sem("m_1a")
        m_2 = sem("m_2")
        m_2a = sem("m_2a")
        m_st = sem("m_st")
        s_bn = sem("s_bn")
        s_bna = sem("s_bna")
        s_deg = sem("s_deg")
        s_dega = sem("s_dega")
        b_a = sem("b_a")
        b_T = sem("b_T")
        b_y = sem("b_y")
        ln = sem("ln")
        ln_v = sem("ln_v")
        ln_r = sem("ln_r")
        s_g = sem("s_g")
        s_res = sem("s_res")
        s_out = sem("s_out")

        VIS = TV + 31

        block = ctx.enter_context(nc.Block())

        def hold(eng, semaphore, value):
            eng.wait_ge(semaphore, value)
            eng.sem_inc(held, 1)

        def nodes(t):
            return t.rearrange("(w p) f -> p w f", p=P)

        def spans(eng, t):
            _, v = nc.values_load_multi_w_load_instructions(
                span[0:1, bass.ds(t * SPAN, SPAN)], engines=[eng.engine], min_val=0, max_val=WINDOWS - 1,
                skip_runtime_bounds_check_because="destinations past the last node were clamped")
            return [(v[2 * i], v[2 * i + 1]) for i in range(RING + 1)]

        def table(eng, tab, t, lo, hi, most):
            _, v = nc.values_load_multi_w_load_instructions(
                bass.at_runtime_partition(tab[0:1, lo:hi], t), engines=[eng.engine], min_val=0, max_val=most,
                skip_runtime_bounds_check_because="the chip packed it from clamped fields")
            return v

        def windows_of(eng, registers, word):
            return [turn_of(eng, r, (word >> (7 * i)) & (P - 1), WINDOWS - 1) for i, r in enumerate(registers)]

        def control(eng):
            eng.wait_ge(s_ctl, 1)
            lim = [(0, TURNS - 2), (2, TURNS), (0, DENSE), (0, DENSE)]
            return [eng.value_load(ctl[0:1, i:i + 1], min_val=a, max_val=b) for i, (a, b) in enumerate(lim)]

        def turn_of(eng, register, turn, most=TURNS - 1):
            eng.reg_mov(register, turn)
            return eng.snap(register, min_val=0, max_val=most)

        @block.sync
        def _(sp):
            for n, t in (("src", src), ("dst", dst)):
                sp.dma_start(raw[n], t.rearrange("(r e) -> r e", r=ROWS)).then_inc(s_raw, 16)
            sp.dma_start(nxt_i[0:ROWS - 1, :], dst[RING * SUPER:].rearrange("(r e) -> r e", e=RING * SUPER)[:, 0:1],
                         allow_slow_non_contiguous=True).then_inc(s_nxt, 16)
            sp.dma_start(nxt_i[ROWS - 1:ROWS, :], dst[E - 1:E].rearrange("(a e) -> a e", a=1)).then_inc(s_nxt, 16)
            sp.wait_ge(s_xz, 1)
            sp.dma_start(xs3[:, 0:WINDOWS - 1, :], nodes(x[0:N - TAIL, :])).then_inc(s_x, 16)
            sp.dma_start(xs3[0:TAIL, WINDOWS - 1, :], x[N - TAIL:N, :]).then_inc(s_x, 16)
            sp.dma_start(be_all[:, :], be.rearrange("(a f) -> a f", a=1).to_broadcast([P, F])).then_inc(s_x, 16)
            sp.wait_ge(s_wz, 1)
            for j in range(4):
                sp.dma_start(We4[j * D:(j + 1) * D, j * F:(j + 1) * F], We).then_inc(s_w, 16)
            sp.dma_start(W1_sb[:, :], W1).then_inc(s_w, 16)
            sp.dma_start(W2_sb[:, :], W2).then_inc(s_w, 16)
            for j, t in enumerate((b1, b2, gamma, beta)):
                sp.dma_start(cols[:, j:j + 1], t.rearrange("(f a) -> f a", a=1)).then_inc(s_w, 16)
            sp.wait_ge(s_span, 5)
            own = span_w[:, :, :].rearrange("r k s -> r (k s)")
            sp.dma_start(span_dram[:, 0:2 * RING], own).then_inc(s_spand, 16)
            sp.dma_start(span_dram[0:TURNS - 1, 2 * RING:SPAN], own[1:ROWS, 0:2]).then_inc(s_spand, 16)
            sp.dma_start(span_dram[TURNS - 1:TURNS, 2 * RING:SPAN], own[0:1, 0:2]).then_inc(s_spand, 16)
            sp.wait_ge(s_spand, 48)
            sp.dma_start(span[:, :], span_dram.rearrange("(a r) s -> a (r s)", a=1)).then_inc(s_spand, 16)
            sp.wait_ge(s_xb, 1)
            sp.dma_start(nodes(xb_dram), agg3[:, :, 0:F]).then_inc(s_tab, 16)
            sp.wait_ge(s_cnt, CG + 1)
            sp.dma_start(cnt_dram.rearrange("(p c) -> p c", p=P), cnt_g[:, :]).then_inc(s_cntd, 16)
            sp.wait_ge(s_cntd, 16)
            sp.dma_start(agg[:, CNT_AT:CNT_AT + SUBS + 1], cnt_dram[0:SUBS + 1].rearrange("(a n) -> a n", a=1).to_broadcast([P, SUBS + 1])
                         ).then_inc(s_cntd, 16)
            ea_v = ea.rearrange("(k p g) d -> k p (g d)", p=P, g=G)
            sp_to = sp.alloc_register("sp_to")

            def load_ea(t, s):
                return sp.dma_start(ea_sb[:, s, :], ea_v[bass.ds(t * RING + s, 1), :, :].rearrange("k p e -> (k p) e")
                                    ).then_inc(ea_in[s], 16)

            def store_counts(t, s, i, to):
                slot = PER * SLOT[s] + i
                hold(sp, visit_copied, t * TV + (PER * s + i + 2))
                sp.dma_start(a_dram[:, :, bass.ds(turn_of(sp, sp_to, to, SUBS + TV - 1), 1), :].rearrange("p h a c -> p h (a c)"),
                             stage_a[:, slot, :, :]).then_inc(stored[slot], 16)

            def turn(t, last):
                row = table(sp, tab_act, t, 0, RING, 4 * DIV * DIV - 1)
                for s in range(RING):
                    for i in range(PER):
                        store_counts(t, s, i, (row[s] >> (10 * i)) & (DIV - 1))
                    if not last:
                        sp.wait_ge(ea_turned, t * RING + (RING + s + 1))
                        load_ea(t + 1, s)

            sp.wait_ge(s_constf, 8)
            for s in range(RING):
                load_ea(0, s)
            sp.wait_ge(s_vis, VIS)
            with sp.Fori(0, TURNS - 1) as t:
                turn(t, False)
            turn(TURNS - 1, True)
            sp.wait_ge(s_g, 1)
            sp.dma_start(nodes(g_dram[0]), agg3[:, :, 0:F]).then_inc(s_tab, 16)
            sp.dma_start(nodes(x1_dram), xs3).then_inc(s_x1, 16)
            sp.wait_ge(s_ctl, 1)
            dense_n = sp.value_load(ctl[0:1, 2:3], min_val=0, max_val=DENSE)
            for i in range(HOTS):
                sp.wait_ge(stored[i], 16 * (TURNS * SLOT.count(i // PER) + 1))
            for h in range(2):
                if h == 1:
                    sp.wait_ge(s_g, 2)
                    sp.dma_start(nodes(g_dram[1]), agg3[:, :, 0:F]).then_inc(s_tab, 16)
                with sp.If(dense_n > 0):
                    with sp.Fori(0, dense_n) as w:
                        for i in range(2):
                            hold(sp, block_used[i], w + dense_n * h + 1)
                            sp.dma_start(blocks[i].rearrange("p n v -> p (n v)"),
                                         a_dram[:, i, bass.ds(w * (P // SUBN), P // SUBN), :].rearrange("p u c -> p (u c)")
                                         ).then_inc(block_in[i], 16)
            hold(sp, dense_acc, dense_n * 2 + 1)
            sp.wait_ge(s_gc, 2)
            sp.dma_start(xs3, nodes(x1_dram)).then_inc(s_x1, 16)
            sp.wait_ge(s_res, GROUPS)
            sp.dma_start(nodes(out[0:N - TAIL, :]), xs3[:, 0:WINDOWS - 1, :]).then_inc(s_out, 16)
            sp.dma_start(out[N - TAIL:N, :], xs3[0:TAIL, WINDOWS - 1, :]).then_inc(s_out, 16)
            sp.wait_ge(s_out, 32)

        @block.gpsimd
        def _(pool):
            nc.gpsimd.memset(xs3[:, WINDOWS - 1, :], 0.0).then_inc(s_xz, 1)
            nc.gpsimd.memset(We4[:, :], 0.0).then_inc(s_wz, 1)
            nc.gpsimd.memset(ident[:, :], 0.0).then_inc(s_iota, 1)
            nc.gpsimd.memset(eps[:, :], EPS).then_inc(s_const, 1)
            nc.gpsimd.iota(node_i[:, :], pattern=[[1, P]], base=0, channel_multiplier=0).then_inc(s_const, 1)
            nc.gpsimd.iota(base_i[:, :], pattern=[[P, WINDOWS]], base=0, channel_multiplier=0).then_inc(s_const, 1)
            nc.gpsimd.iota(sub_i[:, :], pattern=[[1024, SUBS]], base=0, channel_multiplier=0).then_inc(s_const, 1)
            nc.gpsimd.iota(thr_i[:, :], pattern=[[SUBN, CG]], base=0, channel_multiplier=SUBN * CG).then_inc(s_const, 1)
            nc.gpsimd.iota(key_i[:, :], pattern=[[1, SUBW]], base=0, channel_multiplier=0).then_inc(s_const, 1)
            nc.gpsimd.memset(ones[:, :], 1.0).then_inc(s_const, 1)
            nc.gpsimd.memset(pick[:, :], 0.0).then_inc(s_iota, 1)
            nc.gpsimd.memset(zero_b[:, :], 0.0).then_inc(s_const, 1)
            nc.gpsimd.iota(vis_i[:, :], pattern=[[1, TV + 2]], base=-1, channel_multiplier=TV).then_inc(s_const, 1)
            nc.gpsimd.iota(spare_i[:, :], pattern=[[1, TV]], base=SUBS, channel_multiplier=0).then_inc(s_const, 1)
            pool.wait_ge(s_iota, 2)
            nc.gpsimd.affine_select(out=pick[:, :], in_=pick[:, :], compare_op=ALU.not_equal, fill=1.0, base=-(P - 1),
                                    pattern=[[0, P]], channel_multiplier=1).then_inc(s_const, 1)
            nc.gpsimd.affine_select(out=ident[:, :], in_=ident[:, :], compare_op=ALU.not_equal, fill=1.0, base=0,
                                    pattern=[[-1, P]], channel_multiplier=1).then_inc(s_const, 1)
            pool.wait_ge(idx_taken, 2 * RING * G + 1)
            pool.wait_ge(s_ctl, 1)
            hop_turns = pool.value_load(ctl[0:1, 1:2], min_val=2, max_val=TURNS)
            for p in range(3):
                table = [xb_dram, *g_dram][p]
                pool.wait_ge(s_tab, 16 * (p + 1))
                before = 0 if p == 0 else hop_turns * ((p - 1) * RING) + SUPERS
                with pool.Fori(0, TURNS if p == 0 else hop_turns) as t:
                    for s in range(RING):
                        hold(pool, rows_free, t * RING + before + (s + 1))
                        for g in range(G):
                            pool.indirect_dma_start(
                                rows[:, s, g * F:(g + 1) * F], None, table,
                                bass.IndirectOffsetOnAxis(ap=idx[:, s * G + g:s * G + g + 1], axis=0),
                            ).then_inc(gathered[s], 16)

        @block.tensor
        def _(pe):
            pe.wait_ge(s_const, 12)
            pe.wait_ge(s_flt, 2)
            for b in range(RING):
                for g in range(G):
                    if b:
                        pe.wait_ge(idx_taken, 2 * ((b - 1) * G + g + 1))
                    for i, n in enumerate(("src", "dst")):
                        v = flt[n][:, b * SUPER:(b + 1) * SUPER].rearrange("r (q g) -> r g q", g=G)[:, g, :]
                        nc.tensor.transpose(bank[g][:, i * P:i * P + ROWS], v, ident[0:ROWS, 0:ROWS]).then_inc(idx_turned, 1)

            for c in range(RING * G):
                if c >= 3:
                    pe.wait_ge(flat_taken, 2 * (c - 2))
                for i, n in enumerate(("src", "dst")):
                    nc.tensor.transpose(bank[5 + c % 3][:, i * P:i * P + ROWS], flt[n][:, c * P:(c + 1) * P],
                                        ident[0:ROWS, 0:ROWS]).then_inc(flat_turned, 1)
            pe.wait_ge(s_chk, 6)
            pe.wait_ge(idx_taken, 2 * RING * G)
            nc.tensor.matmul(bank[0][:, 0:1], ones[0:ROWS, :], check2[:, 0:1], start=True, stop=True).then_inc(s_tot, 1)
            pe.wait_ge(s_key, 1)
            for i in range(4):
                n = min(512, PAIRS - 1 - i * 512)
                v = last_dst[:, 0:2 * (PAIRS - 1)].rearrange("p (j b) -> p j b", b=2)[:, i * 512:i * 512 + n, 1]
                nc.tensor.matmul(bank[1 + i][:, 0:n], pick[:, :], v, start=True, stop=True).then_inc(s_cntp, 1)

            pe_second, pe_more = (pe.alloc_register(f"pe_{n}") for n in ("second", "more"))
            for r in (pe_second, pe_more):
                pe.reg_mov(r, 0)

            def segment(k, s, span_s, rhs, width):
                def products(rows_of, at):
                    for g in range(G):
                        mm = nc.tensor.matmul(seg_ps[s % 2][:, at:at + width], rows_of[s][:, g, :], rhs(g),
                                              start=(g == 0), stop=(g == G - 1))
                    return mm
                pe.wait_ge(hot_ready, k + 1)
                pe.wait_ge(acc_done, k + (2 if s == 0 else 1))
                products(hot3, 0).then_inc(seg_done, 1)
                first, last = span_s
                with pe.If(last > first):
                    pe.wait_ge(second_hot, pe.snap(pe_second) + 1)
                    products(second3, P).then_inc(second_seg, 1)
                    pe.reg_add(pe_second, pe_second, 1)
                    with pe.If(last > first + 1):
                        with pe.Fori(first + 1, last):
                            pe.wait_ge(more_hot, pe.snap(pe_more) + 1)
                            products(hot3, 0).then_inc(more_seg, 1)
                            pe.reg_add(pe_more, pe_more, 1)
                            hold(pe, more_acc, pe.snap(pe_more) + 1)

            def turn_ea(t, s):
                k = t * RING + s
                pe.wait_ge(ea_in[s], t * 16 + 16)
                pe.wait_ge(eaT_taken, k + 1)
                nc.tensor.transpose(eaT_ps[:, 0:P], ea_sb[:, s, 0:P], ident[:, :])
                nc.tensor.transpose(eaT_ps[0:D, P:2 * P], ea_sb[:, s, P:P + D], ident[:, :]).then_inc(ea_turned, 1)

            def embed(t, s):
                k = t * RING + s
                pe.wait_ge(eaT_taken, k + 2)
                pe.wait_ge(rows_free, k + (RING if s == 0 else RING - 1))
                nc.tensor.matmul(emb_ps[s % 2][:, 0:4 * F], eaT[:, 0:P], We4[:, :], start=True, stop=True)
                nc.tensor.matmul(emb_ps[s % 2][:, 4 * F:5 * F], eaT[0:D, P:2 * P], We4[0:D, 0:F],
                                 start=True, stop=True).then_inc(embedded, 1)

            pe.wait_ge(s_w, 160)
            pe.wait_ge(s_spand, 64)
            pe.wait_ge(s_cnt, CG)
            pe.wait_ge(s_low, 1)
            nc.tensor.matmul(bank[3][:, 0:1], ones[0:ROWS, :], check2[:, 1:2], start=True, stop=True).then_inc(s_tot, 1)
            pe.wait_ge(s_vis, VIS)
            turn_ea(0, 0)
            embed(0, 0)

            def visit(t, s, i, code):
                v = t * TV + (PER * s + i)
                slot = PER * SLOT[s] + i
                to = turn_of(pe, pe_to, (code & 1) * 512, 512)
                opened = turn_of(pe, pe_open, ((code >> 1) & 3) * 512, 1024)
                pe.wait_ge(pair_hot, v + 1)
                pe.wait_ge(visit_copied, v + 1)
                nc.tensor.matmul(count_ps[:, bass.ds(opened, SUBW)], zero_b[:, :], key_hot[:, 2 * slot * SUBW:(2 * slot + 1) * SUBW],
                                 start=True, stop=False, skip_group_check=True)
                for c in range(2):
                    at = slot * 2 + c
                    mm = nc.tensor.matmul(count_ps[:, bass.ds(to, SUBW)], low_hot[:, at * P:(at + 1) * P],
                                          key_hot[:, at * SUBW:(at + 1) * SUBW], start=False, stop=(c == 1), skip_group_check=True)
                mm.then_inc(visit_done, 1)

            pe_windows = [[pe.alloc_register(f"pe_{n}{s}") for n in ("first", "last")] for s in range(RING)]
            pe_to = pe.alloc_register("pe_to")
            pe_open = pe.alloc_register("pe_open")

            def turn(t, last):
                row = table(pe, tab_pe, t, 0, RING, 64 * P * P - 1)
                for s in range(RING):
                    codes, span_s = row[s] >> 14, windows_of(pe, pe_windows[s], row[s])
                    following = (t, s + 1) if s < RING - 1 else (t + 1, 0)
                    if s < RING - 1 or not last:
                        turn_ea(*following)
                    visit(t, s, 0, codes & 7)
                    if s < RING - 1 or not last:
                        embed(*following)
                    visit(t, s, 1, (codes >> 3) & 7)
                    pe.wait_ge(relu_done, t * RING + s + 1)
                    segment(t * RING + s, s, span_s, lambda g: msg3[s][:, g, :], FD)

            with pe.Fori(0, TURNS - 1) as t:
                turn(t, False)
            turn(TURNS - 1, True)

            def mlp(j, nw):
                c = nw * P
                pe.wait_ge(m_h, j + 1)
                pe.wait_ge(m_Tc, j + 1)
                for i in range(nw):
                    tr = nc.tensor.transpose(bank[4][0:F, i * P:(i + 1) * P], hs[:, i, :], ident[:, :])
                tr.then_inc(m_T, 1)
                pe.wait_ge(m_Tc, j + 2)
                pe.wait_ge(m_1a, j + 1)
                nc.tensor.matmul(bank[5][0:F, 0:c], W1_sb[:, :], hT[:, 0:c], start=True, stop=True).then_inc(m_1, 1)
                pe.wait_ge(m_1a, j + 2)
                pe.wait_ge(m_2a, j + 1)
                nc.tensor.matmul(bank[6][0:F, 0:c], W2_sb[:, :], hid[:, 0:c], start=True, stop=True).then_inc(m_2, 1)

            with pe.Fori(0, GROUPS - 1) as j:
                mlp(j, GROUP)
            mlp(GROUPS - 1, LAST)

            def back(j, nw):
                pe.wait_ge(b_a, j + 1)
                pe.wait_ge(b_y, j + 1)
                for i in range(nw):
                    tr = nc.tensor.transpose(bank[4][:, i * F:(i + 1) * F], yT[:, i * P:(i + 1) * P], ident[0:F, 0:F])
                tr.then_inc(b_T, 1)

            with pe.Fori(0, GROUPS - 1) as j:
                back(j, GROUP)
            back(GROUPS - 1, LAST)

            first_turn, hop_turns, dense_n, dense_t = control(pe)
            pe_turn = pe.alloc_register("pe_turn")
            hold(pe, s_cut, 1)
            for h in range(2):
                def dense_part(w, lo, hi):
                    for v in range(lo, hi):
                        half, i = divmod(v, WINDOWS // 2)
                        if v == 0:
                            pe.wait_ge(dense_acc, w + dense_n * h + 1)
                        if i == 0:
                            pe.wait_ge(block_in[half], (w + dense_n * h) * 16 + 16)
                        mm = nc.tensor.matmul(bank[5][:, 0:F], blocks[half][:, :, i],
                                              xs3[:, v, :], start=(v == 0), stop=(v == WINDOWS - 1))
                        if i == WINDOWS // 2 - 1:
                            mm.then_inc(block_used[half], 1)
                    if hi == WINDOWS:
                        nc.tensor.matmul(bank[5][:, 511:512], zero_b[:, :], zero_b[:, 0:1], start=False, stop=True,
                                         skip_group_check=True).then_inc(dense_done, 1)

                def hop_turn(t, dense):
                    sp_t = spans(pe, turn_of(pe, pe_turn, t + first_turn))
                    for s in range(RING):
                        if dense:
                            n = -(-WINDOWS // RING)
                            dense_part(t, n * s, min(n * (s + 1), WINDOWS))
                        pe.wait_ge(gathered[s], (t + hop_turns * h) * (16 * G) + 16 * G * (TURNS + 1))
                        segment((t + hop_turns * h) * RING + (SUPERS + s), s, sp_t[s], lambda g: rows[:, s, g * F:(g + 1) * F], F)

                pe.wait_ge(s_gc, h + 1)
                with pe.If(dense_t > 0):
                    with pe.Fori(0, dense_t) as t:
                        hop_turn(t, True)
                with pe.If(hop_turns > dense_t):
                    with pe.Fori(dense_t, hop_turns) as t:
                        hop_turn(t, False)
                with pe.If(dense_n > dense_t):
                    with pe.Fori(dense_t, dense_n) as w:
                        dense_part(w, 0, WINDOWS)

        @block.scalar
        def _(act):
            def take(t, s):
                k = t * RING + s
                act.wait_ge(embedded, k + 1)
                act.wait_ge(ea_turned, k + RING + 1)
                nc.scalar.copy(eaT[:, 0:P], eaT_ps[:, 0:P])
                nc.scalar.copy(eaT[0:D, P:2 * P], eaT_ps[0:D, P:2 * P]).then_inc(eaT_taken, 1)

            for c in range(RING * G):
                act.wait_ge(flat_turned, 2 * (c + 1))
                if c == 0:
                    act.wait_ge(s_flt, 2)
                for i, v in enumerate((src_ci, dst_ci)):
                    to = v[:, 0:CHUNKS].rearrange("q (r c) -> q c r", c=RING * G)[:, c, :]
                    nc.scalar.copy(to, bank[5 + c % 3][:, i * P:i * P + ROWS]).then_inc(flat_taken, 1)
            act.sem_inc(eaT_taken, 1)
            act.sem_inc(visit_copied, 1)
            for i in range(HOTS):
                act.sem_inc(stored[i], 16)
            act.sem_inc(m_1a, 1)
            act.sem_inc(m_2a, 1)
            take(0, 0)

            act_from = act.alloc_register("act_from")

            def take_counts(t, s, i, par):
                v = t * TV + (PER * s + i)
                slot, uses = PER * SLOT[s] + i, SLOT.count(SLOT[s])
                hold(act, stored[slot], t * (16 * uses) + 16 * (1 + SLOT[:s].count(SLOT[s])))
                act.wait_ge(visit_done, v + (2 * PER + 1))
                at = turn_of(act, act_from, par * 512, 512)
                nc.scalar.copy(stage_a[:, slot, :, :].rearrange("p h (d v) -> p h d v", d=SUBN),
                               count_ps[:, bass.ds(at, SUBW)].rearrange("p (d h v) -> p h d v", d=SUBN, h=2)).then_inc(visit_copied, 1)

            def turn(t, last):
                row = table(act, tab_act, t, 0, RING, 4 * DIV * DIV - 1)
                for s in range(RING):
                    word = row[s]
                    if s < RING - 1:
                        take(t, s + 1)
                    elif not last:
                        take(t + 1, 0)
                    take_counts(t, s, 0, (word >> 20) & 1)
                    act.wait_ge(rows_free, t * RING + (RING + s + 1))
                    nc.scalar.activation(msg3[s][:, :, 0:F], msg3[s][:, :, 0:F], ACT.Relu).then_inc(relu_done, 1)
                    take_counts(t, s, 1, (word >> 21) & 1)

            act.wait_ge(s_vis, VIS)
            with act.Fori(0, TURNS - 1) as t:
                turn(t, False)
            turn(TURNS - 1, True)

            act.wait_ge(s_deg, 1)
            nc.scalar.activation(root[:, :], deg[:, :], ACT.Sqrt).then_inc(s_dega, 1)

            def mlp(j, nw):
                c = nw * P
                act.wait_ge(m_1, j + 2)
                act.wait_ge(m_2, j + 1)
                nc.scalar.activation(hid[:, 0:c], bank[5][0:F, 0:c], ACT.Relu, bias=cols[:, 0:1]).then_inc(m_1a, 1)
                act.wait_ge(m_2, j + 2)
                nc.scalar.activation(h2T[:, bass.ds(j * GN, c)], bank[6][0:F, 0:c], ACT.Identity, bias=cols[:, 1:2]).then_inc(m_2a, 1)

            for i in range(HOTS):
                act.wait_ge(stored[i], 16 * (TURNS * SLOT.count(i // PER) + 1))
            act.sem_inc(m_2, 1)
            act.wait_ge(s_w, 160)
            with act.Fori(0, GROUPS - 1) as j:
                mlp(j, GROUP)
            mlp(GROUPS - 1, LAST)

            act.wait_ge(s_bn, 1)
            nc.scalar.activation(bn[:, 0:1], mv[:, 1:2], ACT.Sqrt, bias=eps[0:F, :]).then_inc(s_bna, 1)
            act.sem_inc(b_T, 1)
            act.wait_ge(s_bn, 5)

            def scale(j, nw):
                c = nw * P
                act.wait_ge(b_T, j + 1)
                nc.scalar.activation(yT[:, 0:c], h2T[:, bass.ds(j * GN, c)], ACT.Relu, bias=bn[:, 3:4], scale=bn[:, 2:3]).then_inc(b_a, 1)

            def ln_root(n):
                act.wait_ge(ln_v, n + 1)
                nc.scalar.activation(lroot[:, :], lmv[:, :, 1], ACT.Sqrt, bias=eps[:, :]).then_inc(ln_r, 1)

            with act.Fori(0, GROUPS - 1) as j:
                scale(j, GROUP)
                ln_root(j)
            scale(GROUPS - 1, LAST)
            ln_root(GROUPS - 1)
            with act.Fori(0, GROUPS) as j:
                ln_root(j + GROUPS)

        @block.vector
        def _(dve):
            dve.sem_inc(rows_free, RING)
            dve.sem_inc(visit_done, 2 * PER)
            dve.sem_inc(block_used[0], 1)
            dve.sem_inc(block_used[1], 1)
            dve.sem_inc(dense_acc, 1)
            dve.sem_inc(ea_turned, RING)
            dve.sem_inc(embedded, 1)
            dve.sem_inc(acc_done, 2)
            dve.sem_inc(more_acc, 1)
            dve.sem_inc(m_Tc, 1)
            dve.sem_inc(b_y, 1)
            nc.vector.memset(msg[:, :, :], 1.0).then_inc(s_constf, 1)
            nc.vector.memset(lmv[:, :, :], 1.0).then_inc(s_constf, 1)
            dve.wait_ge(s_raw, 32)
            for n in ("dst", "src"):
                nc.vector.tensor_copy(flt[n], raw[n]).then_inc(s_flt, 1)
            dve.wait_ge(s_flt, 1)
            d3 = flt["dst"].rearrange("r (k e) -> r k e", e=SUPER)
            nc.vector.tensor_reduce(span_f[:, :, 0], d3, AX_X, ALU.min).then_inc(s_span, 1)
            nc.vector.tensor_reduce(span_f[:, :, 1], d3, AX_X, ALU.max).then_inc(s_span, 1)
            dve.wait_ge(s_span, 2)
            nc.vector.tensor_scalar(span_f[:, :, :], span_f[:, :, :], float(N - 1), None, ALU.min).then_inc(s_span, 1)
            dve.wait_ge(s_span, 3)
            nc.vector.tensor_copy(span_n[:, :, :], span_f[:, :, :]).then_inc(s_span, 1)
            dve.wait_ge(s_span, 4)
            nc.vector.tensor_scalar(span_w[:, :, :], span_n[:, :, :], 7, None, ALU.arith_shift_right).then_inc(s_span, 1)
            d = flt["dst"]
            W = RING * SUPER
            dve.wait_ge(s_nxt, 32)
            nc.vector.tensor_copy(nxt[:, :], nxt_i[:, :]).then_inc(s_chk, 1)
            dve.wait_ge(s_flt, 2)
            nc.vector.tensor_tensor(agg[0:ROWS, 0:W - 1], d[:, 0:W - 1], d[:, 1:W], ALU.is_gt).then_inc(s_chk, 1)
            dve.wait_ge(s_chk, 2)
            nc.vector.tensor_reduce(checks[:, 0:1], agg[0:ROWS, 0:W - 1], AX_X, ALU.max).then_inc(s_chk, 1)
            nc.vector.tensor_tensor(checks[:, 1:2], d[:, W - 1:W], nxt[:, :], ALU.is_gt).then_inc(s_chk, 1)
            nc.vector.tensor_reduce(checks[:, 2:3], span_f[:, :, 1], AX_X, ALU.max).then_inc(s_chk, 1)
            dve.wait_ge(s_chk, 5)
            nc.vector.tensor_tensor(check2[:, 0:1], checks[:, 0:1], checks[:, 1:2], ALU.add).then_inc(s_chk, 1)
            dve.wait_ge(s_x, 48)
            nc.vector.tensor_tensor(agg3[:, :, 0:F], xs3, be_all[:, :].unsqueeze(1).to_broadcast([P, WINDOWS, F]),
                                    ALU.add).then_inc(s_xb, 1)
            dve.wait_ge(s_const, 12)
            nc.vector.tensor_copy(node[:, :], node_i[:, :]).then_inc(s_constf, 1)
            nc.vector.tensor_copy(base[:, :], base_i[:, :]).then_inc(s_constf, 1)
            nc.vector.tensor_copy(thr[:, :], thr_i[:, :]).then_inc(s_constf, 1)
            nc.vector.tensor_copy(sub_base[:, :], sub_i[:, :]).then_inc(s_constf, 1)
            nc.vector.tensor_copy(vis[:, :], vis_i[:, :]).then_inc(s_constf, 1)
            nc.vector.tensor_copy(spare[:, :], spare_i[:, :]).then_inc(s_constf, 1)
            srcv = src_all[:, :].rearrange("q (r c) -> q c r", c=RING * G)
            dstv = dst_all[:, :].rearrange("q (r c) -> q c r", c=RING * G)
            for b in range(RING):
                for g in range(G):
                    for i, v in enumerate((srcv, dstv)):
                        dve.wait_ge(idx_turned, 2 * (b * G + g + 1))
                        nc.vector.tensor_copy(v[:, b * G + g, :],
                                              bank[g][:, i * P:i * P + ROWS]).then_inc(idx_taken, 1)
            dve.wait_ge(idx_taken, 2 * RING * G)
            nc.vector.tensor_copy(idx[:, :], src_all[:, 0:RING * G]).then_inc(idx_taken, 1)
            dve.wait_ge(s_tot, 1)
            nc.vector.tensor_scalar(okay[:, :], bank[0][:, 0:1], 0.0, None, ALU.is_equal).then_inc(s_ctlf, 1)
            dve.wait_ge(s_tab, 16)
            dve.wait_ge(flat_taken, 2 * RING * G)
            tmp = [agg[:, i * C2:i * C2 + CHUNKS] for i in range(3)]
            tmi = [v.bitcast(I32) for v in tmp]
            sc, dc = src_ci[:, 0:CHUNKS], dst_ci[:, 0:CHUNKS]
            nc.vector.tensor_copy(last_dst[:, 0:CHUNKS], dc).then_inc(s_key, 1)
            dve.wait_ge(s_key, 1)
            nc.vector.tensor_scalar(tmi[0], sc, 7, None, ALU.arith_shift_right).then_inc(s_key, 1)
            nc.vector.tensor_scalar(tmi[1], sc, P - 1, None, ALU.bitwise_and).then_inc(s_key, 1)
            dve.wait_ge(s_key, 3)
            nc.vector.tensor_copy(src_c[:, 0:CHUNKS], tmi[1]).then_inc(s_key, 1)
            dve.wait_ge(s_cntp, 4)
            nc.vector.tensor_scalar(tmi[2], dc, SUBN - 1, None, ALU.bitwise_and).then_inc(s_key, 1)
            dve.wait_ge(s_key, 5)
            nc.vector.tensor_scalar(tmi[1], dc, 2, 10, ALU.arith_shift_right, ALU.logical_shift_left).then_inc(s_key, 1)
            dve.wait_ge(s_key, 6)
            nc.vector.tensor_tensor(dst_c[:, 0:CHUNKS], tmi[0], tmi[1], ALU.add).then_inc(s_key, 1)
            dve.wait_ge(s_key, 7)
            nc.vector.scalar_tensor_tensor(out=dst_c[:, 0:CHUNKS], in0=tmi[2], scalar=float(WINDOWS), in1=dst_c[:, 0:CHUNKS],
                                           op0=ALU.mult, op1=ALU.add).then_inc(s_key, 1)
            nc.vector.memset(src_c[:, CHUNKS:], 0.0).then_inc(s_key, 1)
            nc.vector.memset(dst_c[:, CHUNKS:], -1.0).then_inc(s_key, 1)
            nc.vector.tensor_copy(key_no, key_i[:, :]).then_inc(s_key, 1)
            dve.wait_ge(s_key, 11)
            for i in range(4):
                n = min(512, PAIRS - 1 - i * 512)
                nc.vector.tensor_copy(agg[:, i * 512:i * 512 + n], bank[1 + i][:, 0:n]).then_inc(s_zero, 1)
            dve.wait_ge(s_constf, 8)
            dve.wait_ge(s_zero, 4)
            for c in range(CG):
                if c >= 2:
                    dve.wait_ge(s_cnt, c - 1)
                junk = 2048 * (1 + c % 2)
                nc.vector.tensor_scalar(agg[:, junk:junk + PAIRS - 1], agg[:, 0:PAIRS - 1], thr[:, c:c + 1], None,
                                        ALU.is_lt, ALU.add, accum_out=cnt_f[:, c:c + 1]).then_inc(s_cnt, 1)
            dve.wait_ge(s_cnt, CG)
            dve.wait_ge(s_ctlf, 1)
            nc.vector.tensor_scalar(cnt_g[:, :], cnt_f[:, :], okay[:, :], None, ALU.mult).then_inc(s_cnt, 1)
            ends = agg[:, END_AT:END_AT + SUBS]
            dve.wait_ge(s_cntd, 32)
            nc.vector.scalar_tensor_tensor(out=ends, in0=sub_base[:, :], scalar=1.0 / 1024, in1=agg[:, CNT_AT + 1:CNT_AT + SUBS + 1],
                                           op0=ALU.mult, op1=ALU.add).then_inc(s_vis, 1)
            dve.wait_ge(s_vis, 1)
            nc.vector.tensor_scalar(agg[:, 0:DENSE], ends.rearrange("p (d u) -> p d u", u=P // SUBN)[:, :, P // SUBN - 1],
                                    VISITS - 0.5, None, ALU.is_lt, ALU.add, accum_out=dense_f[:, 0:1]).then_inc(s_vis, 1)
            dve.wait_ge(s_vis, 2)
            nc.vector.tensor_tensor(dense_f[:, 1:2], dense_f[:, 0:1], okay[:, :], ALU.mult).then_inc(s_vis, 1)
            dve.wait_ge(s_vis, 3)
            nc.vector.tensor_scalar(lim[:, :], dense_f[:, 1:2], float(P), None, ALU.mult).then_inc(s_vis, 1)
            dve.wait_ge(s_vis, 4)
            nc.vector.tensor_tensor(check2[:, 1:2], checks[:, 2:3], lim[0:ROWS, :], ALU.is_lt).then_inc(s_low, 1)
            for c in range(TV + 2):
                if c >= 2:
                    dve.wait_ge(s_vis, c + 3)
                junk = 1024 * (c % 2)
                nc.vector.tensor_scalar(agg[0:ROWS, junk + DENSE:junk + DENSE + SUBS], ends[0:ROWS, :], vis[:, c:c + 1], None,
                                        ALU.is_lt, ALU.add, accum_out=sub[:, c:c + 1]).then_inc(s_vis, 1)
            n = TV + 6
            dve.wait_ge(s_vis, n)
            nc.vector.memset(sub[0:1, 0:1], -1.0).then_inc(s_vis, 1)
            dve.wait_ge(s_vis, n + 1)
            own = sub[:, 1:TV + 1]
            new, fin, low, par, code, to = (fields[:, i, :] for i in range(6))
            nc.vector.tensor_tensor(new, own, sub[:, 0:TV], ALU.is_gt).then_inc(s_vis, 1)
            nc.vector.tensor_tensor(fields[:, 6, :], sub[:, 2:TV + 2], own, ALU.is_gt).then_inc(s_vis, 1)
            nc.vector.tensor_scalar(low, own, float(SUBS - 1), None, ALU.min).then_inc(s_vis, 1)
            nc.vector.tensor_copy(sub_n[:, :], own).then_inc(s_vis, 1)
            nc.vector.tensor_tensor(fields[:, 7, :], own, spare[:, :], ALU.subtract).then_inc(s_vis, 1)
            nc.vector.tensor_copy(packed[:, 3, :, :], span_w[:, :, :]).then_inc(s_vis, 1)
            dve.wait_ge(s_vis, n + 7)
            nc.vector.tensor_scalar(par_n[:, :], sub_n[:, :], 1, None, ALU.bitwise_and).then_inc(s_vis, 1)
            nc.vector.scalar_tensor_tensor(out=fin, in0=own, scalar=float(SUBS), in1=fields[:, 6, :], op0=ALU.is_lt, op1=ALU.mult).then_inc(s_vis, 1)
            dve.wait_ge(s_vis, n + 9)
            nc.vector.tensor_copy(par, par_n[:, :]).then_inc(s_vis, 1)
            nc.vector.tensor_tensor(to, fields[:, 7, :], fin, ALU.mult).then_inc(s_vis, 1)
            dve.wait_ge(s_vis, n + 11)
            nc.vector.scalar_tensor_tensor(out=code, in0=par, scalar=-2.0, in1=new, op0=ALU.add, op1=ALU.mult).then_inc(s_vis, 1)
            nc.vector.tensor_tensor(fields[:, 6, :], to, spare[:, :], ALU.add).then_inc(s_vis, 1)
            dve.wait_ge(s_vis, n + 13)
            nc.vector.tensor_scalar(fields[:, 7, :], code, 2.0, 4.0, ALU.mult, ALU.add).then_inc(s_vis, 1)
            dve.wait_ge(s_vis, n + 14)
            nc.vector.tensor_tensor(code, fields[:, 7, :], par, ALU.add).then_inc(s_vis, 1)

            def two(field, i):
                return field.rearrange("r (s i) -> r s i", i=PER)[:, :, i]

            def pack(out, a, b, unit):
                return nc.vector.scalar_tensor_tensor(out=out, in0=b, scalar=float(unit), in1=a, op0=ALU.mult, op1=ALU.add)

            dve.wait_ge(s_vis, n + 15)
            pack(packed[:, 0, :, 0], two(low, 0), two(low, 1), DIV).then_inc(s_vis, 1)
            pack(packed[:, 0, :, 1], packed[:, 3, :, 0], packed[:, 3, :, 1], P).then_inc(s_vis, 1)
            pack(packed[:, 1, :, 0], two(code, 0), two(code, 1), 8).then_inc(s_vis, 1)
            pack(packed[:, 2, :, 0], two(par, 0), two(par, 1), 2).then_inc(s_vis, 1)
            pack(packed[:, 2, :, 1], two(fields[:, 6, :], 0), two(fields[:, 6, :], 1), DIV).then_inc(s_vis, 1)
            dve.wait_ge(s_vis, n + 20)
            pack(packed[:, 1, :, 1], packed[:, 2, :, 1], packed[:, 2, :, 0], DIV * DIV).then_inc(s_vis, 1)
            nc.vector.tensor_copy(tab_dve[:, 0:TV], packed[:, 0, :, :].rearrange("r s i -> r (s i)")).then_inc(s_vis, 1)
            pack(code[:, 0:RING], packed[:, 0, :, 1], packed[:, 1, :, 0], P * P).then_inc(s_vis, 1)
            dve.wait_ge(s_vis, n + 23)
            nc.vector.tensor_copy(tab_pe[:, 0:RING], code[:, 0:RING]).then_inc(s_vis, 1)
            nc.vector.tensor_copy(tab_act[:, 0:RING], packed[:, 1, :, 1]).then_inc(s_vis, 1)
            assert n + 25 == VIS
            dve.wait_ge(s_tot, 2)
            nc.vector.tensor_scalar(ctl_f[:, 0:1], bank[3][0:1, 0:1], float(TURNS - 2), None, ALU.min).then_inc(s_ctlf, 1)
            nc.vector.tensor_copy(ctl_f[:, 2:3], dense_f[0:1, 1:2]).then_inc(s_ctlf, 1)
            dve.wait_ge(s_ctlf, 3)
            nc.vector.tensor_scalar(ctl_f[:, 1:2], ctl_f[:, 0:1], -1.0, float(TURNS), ALU.mult, ALU.add).then_inc(s_ctlf, 1)
            dve.wait_ge(s_ctlf, 4)
            nc.vector.tensor_tensor(ctl_f[:, 3:4], ctl_f[:, 1:2], ctl_f[:, 2:3], ALU.min).then_inc(s_ctlf, 1)
            dve.wait_ge(s_ctlf, 5)
            nc.vector.tensor_copy(ctl[:, :], ctl_f[:, 0:4]).then_inc(s_ctl, 1)
            nc.vector.memset(agg[:, :], 0.0).then_inc(s_zero, 1)
            dve.wait_ge(s_spand, 64)
            dve.wait_ge(s_zero, 5)
            dve.wait_ge(s_vis, VIS)
            dve.wait_ge(idx_taken, 2 * RING * G + 1)
            first_turn, hop_turns, dense_n, dense_t = control(dve)
            dve_turn = dve.alloc_register("dve_turn")
            dve_win = dve.alloc_register("dve_win")
            dve_after = dve.alloc_register("dve_after")

            def stage(t, s):
                return nc.vector.tensor_copy(idx[:, s * G:(s + 1) * G], src_all[:, bass.ds(t * (RING * G) + s * G, G)])

            dve_sub = dve.alloc_register("dve_sub")
            dve_chunk = dve.alloc_register("dve_chunk")

            def pair_rows(t, s, subs):
                for i in range(PER):
                    v, w = t * TV + (PER * s + i), (subs >> (10 * i)) & (DIV - 1)
                    wb = turn_of(dve, dve_sub, w, SUBS - 1)
                    chunk = turn_of(dve, dve_chunk, (v - wb) * 2, 2 * (PAIRS - 1))
                    dve.wait_ge(visit_done, v + 1)
                    for c in range(2):
                        at = (PER * SLOT[s] + i) * 2 + c
                        nc.vector.tensor_scalar(low_hot[:, at * P:(at + 1) * P], key_no[:, 0:P], src_c[:, bass.ds(chunk + c, 1)], None, ALU.is_equal)
                        th = nc.vector.tensor_scalar(key_hot[:, at * SUBW:(at + 1) * SUBW], key_no, sub_base[:, bass.ds(wb, 1)],
                                                     dst_c[:, bass.ds(chunk + c, 1)], ALU.add, ALU.is_equal)
                    th.then_inc(pair_hot, 1)

            dve_second, dve_more, dve_at = (dve.alloc_register(f"dve_{n}") for n in ("second", "more", "at"))
            for r in (dve_second, dve_more):
                dve.reg_mov(r, 0)

            def one_hot(t, s, w, rows_of):
                d = dst_all[:, bass.ds(t * (RING * G) + s * G, G)].unsqueeze(2).to_broadcast([P, G, P])
                return nc.vector.scalar_tensor_tensor(
                    out=rows_of[s], in0=d, scalar=base[:, bass.ds(w, 1)],
                    in1=node[:, :].unsqueeze(1).to_broadcast([P, G, P]), op0=ALU.subtract, op1=ALU.is_equal)

            def one_hots(t, s, span_s):
                first, last = span_s
                one_hot(t, s, first, hot3).then_inc(hot_ready, 1)
                with dve.If(last > first):
                    one_hot(t, s, turn_of(dve, dve_at, first + 1, WINDOWS - 1), second3).then_inc(second_hot, 1)

            def accumulate(k, t, s, span_s, width):
                def add(w, n=1):
                    a = agg[:, bass.ds(w * FD, n * FD)].rearrange("p (w f) -> p w f", f=FD)[:, :, 0:width]
                    by = seg_ps[s % 2][:, 0:n * P].rearrange("p (w f) -> p w f", f=P)[:, :, 0:width]
                    return nc.vector.tensor_tensor(a, a, by, ALU.add)
                first, last = span_s
                dve.wait_ge(seg_done, k + 1)
                hold(dve, acc_done, k + 2)
                with dve.If(last > first):
                    dve.wait_ge(second_seg, dve.snap(dve_second) + 1)
                    dve.reg_add(dve_second, dve_second, 1)
                    add(turn_of(dve, dve_at, first, WINDOWS - 2), 2).then_inc(acc_done, 1)
                    with dve.If(last > first + 1):
                        hold(dve, acc_done, k + 3)
                        with dve.Fori(first + 1, last) as w:
                            n = dve.snap(dve_more)
                            at = turn_of(dve, dve_at, w + 1, WINDOWS - 1)
                            one_hot(t, s, at, hot3).then_inc(more_hot, 1)
                            dve.wait_ge(more_seg, n + 1)
                            add(at).then_inc(more_acc, 1)
                            dve.reg_add(dve_more, dve_more, 1)
                            hold(dve, more_acc, n + 2)
                with dve.Else():
                    add(first).then_inc(acc_done, 1)

            def combine(t, s, after=None):
                dve.wait_ge(gathered[s], t * (16 * G) + 16 * G)
                stage(t + 1 if after is None else after, s)
                dve.wait_ge(embedded, t * RING + (s + 2))
                nc.vector.tensor_tensor(msg3[s][:, :, 0:F], rows[:, s, :].rearrange("p (g f) -> p g f", f=F),
                                        emb_ps[s % 2][:, 0:G * F].rearrange("p (g f) -> p g f", f=F),
                                        ALU.add).then_inc(rows_free, 1)

            dve_windows = [[dve.alloc_register(f"dve_{n}{s}") for n in ("first", "last")] for s in range(RING)]

            def record(t, s):
                subs, word = table(dve, tab_dve, t, 2 * s, 2 * s + 2, DIV * DIV - 1)
                return subs, windows_of(dve, dve_windows[s], word)

            subs, windows = record(0, 0)
            one_hots(0, 0, windows)
            combine(0, 0)
            pair_rows(0, 0, subs)

            def turn(t, last, final=False):
                row = table(dve, tab_dve, t, PER, TV, DIV * DIV - 1)
                first = [dve.snap(r, min_val=0, max_val=WINDOWS - 1) for r in dve_windows[0]]
                recs = [(None, first)] + [(row[2 * s - 2], windows_of(dve, dve_windows[s], row[2 * s - 1])) for s in range(1, RING)]
                for s in range(RING):
                    if s < RING - 1 or not last:
                        tn, sn = (t, s + 1) if s < RING - 1 else (t + 1, 0)
                        subs, windows = recs[s + 1] if s < RING - 1 else record(tn, 0)
                        one_hots(tn, sn, windows)
                        combine(tn, sn, first_turn if last or (final and s == RING - 1) else None)
                        pair_rows(tn, sn, subs)
                    accumulate(t * RING + s, t, s, recs[s][1], FD)

            with dve.Fori(0, TURNS - 2) as t:
                turn(t, False)
            turn(TURNS - 2, False, final=True)
            turn(TURNS - 1, True)
            dve.wait_ge(acc_done, SUPERS + 2)
            nc.vector.tensor_scalar(span[:, :], span[:, :], ctl_f[:, 2:3], None, ALU.max).then_inc(s_cut, 1)
            dve.wait_ge(s_cut, 1)
            nc.vector.tensor_scalar(deg[:, :], agg3[:, :, F], 1.0, None, ALU.add).then_inc(s_deg, 1)
            dve.wait_ge(s_deg, 1)
            nc.vector.reciprocal(inv[:, :], deg[:, :]).then_inc(s_deg, 1)
            dve.wait_ge(s_dega, 1)
            nc.vector.reciprocal(dis[:, :], root[:, :]).then_inc(s_deg, 1)

            def mlp(j, nw):
                c = nw * P
                dve.wait_ge(m_T, j + 1)
                nc.vector.tensor_tensor(hs[:, 0:nw, :],
                                        agg[:, bass.ds(j * (GROUP * FD), nw * FD)].rearrange("p (w f) -> p w f", f=FD)[:, :, 0:F],
                                        xs[:, bass.ds(j * (GROUP * F), nw * F)].rearrange("p (w f) -> p w f", f=F),
                                        ALU.add).then_inc(m_h, 1)
                dve.wait_ge(m_T, j + 2)
                dve.wait_ge(m_1, j + 1)
                nc.vector.tensor_copy(hT[:, 0:c], bank[4][0:F, 0:c]).then_inc(m_Tc, 1)

            dve.sem_inc(m_1, 1)
            dve.sem_inc(m_T, 1)
            with dve.Fori(0, GROUPS - 1) as j:
                mlp(j, GROUP)
            mlp(GROUPS - 1, LAST)
            for c in range(N // BN):
                dve.wait_ge(m_2a, 1 + min(GROUPS, -(-(c + 1) * BN // GN)))
                nc.vector.bn_stats(stats[:, c, :], h2T[:, c * BN:(c + 1) * BN]).then_inc(m_st, 1)
            dve.wait_ge(m_st, N // BN)
            nc.vector.bn_aggr(mv[:, :], stats2).then_inc(s_bn, 1)
            dve.wait_ge(s_bna, 1)
            nc.vector.reciprocal(bn[:, 1:2], bn[:, 0:1]).then_inc(s_bn, 1)
            dve.wait_ge(s_bn, 2)
            nc.vector.tensor_tensor(bn[:, 2:3], bn[:, 1:2], cols[:, 2:3], ALU.mult).then_inc(s_bn, 1)
            dve.wait_ge(s_bn, 3)
            nc.vector.tensor_tensor(bnt[:, :], mv[:, 0:1], bn[:, 2:3], ALU.mult).then_inc(s_bn, 1)
            dve.wait_ge(s_bn, 4)
            nc.vector.tensor_tensor(bn[:, 3:4], cols[:, 3:4], bnt[:, :], ALU.subtract).then_inc(s_bn, 1)

            CH = 5

            def layer_norm(j, nw, m, done):
                w0 = j * GROUP
                xw = [xs[:, bass.ds((w0 + i) * F, F)] for i in range(nw)]
                hold(dve, ln, m * CH + 1)
                for i in range(nw):
                    st = nc.vector.bn_stats(lst[:, i, :], xw[i])
                st.then_inc(ln, 1)
                hold(dve, ln, m * CH + 2)
                for i in range(nw):
                    ag = nc.vector.bn_aggr(lmv[:, i, :], lst[:, i, :])
                ag.then_inc(ln_v, 1)
                dve.wait_ge(ln_r, m + 1)
                nc.vector.reciprocal(lrs[:, :], lroot[:, :]).then_inc(ln, 1)
                dve.wait_ge(ln, m * CH + 3)
                for i in range(nw):
                    ts = nc.vector.tensor_scalar(xw[i], xw[i], lmv[:, i, 0:1], lrs[:, i:i + 1], ALU.subtract, ALU.mult)
                ts.then_inc(ln, 1)
                if done is not None:
                    dve.wait_ge(ln, m * CH + 4)

            def first_norm(j, nw):
                w0 = j * GROUP
                xw = xs[:, bass.ds(w0 * F, nw * F)]
                dve.wait_ge(b_T, j + 2)
                nc.vector.tensor_tensor(xw, xw, bank[4][:, 0:nw * F], ALU.add).then_inc(b_y, 1)
                hold(dve, b_y, j + 2)
                layer_norm(j, nw, j, True)
                av = agg[:, bass.ds(w0 * FD, nw * FD)].rearrange("p (w f) -> p w f", f=FD)[:, :, 0:F]
                nc.vector.tensor_tensor(av, xw.rearrange("p (w f) -> p w f", f=F),
                                        dis[:, bass.ds(w0, nw)].unsqueeze(2).to_broadcast([P, nw, F]),
                                        ALU.mult).then_inc(ln, 2)

            dve.sem_inc(ln, 1)
            dve.wait_ge(s_deg, 3)
            with dve.Fori(0, GROUPS - 1) as j:
                first_norm(j, GROUP)
            first_norm(GROUPS - 1, LAST)
            dve.wait_ge(ln, GROUPS * CH + 1)
            dve.sem_inc(s_g, 1)

            for h in range(2):
                dve.wait_ge(s_tab, 16 * (h + 2))
                dve.wait_ge(s_x1, 16)
                nc.vector.tensor_copy(xs3, agg3[:, :, 0:F]).then_inc(s_gc, 1)

                def add_dense(w):
                    a = agg[:, bass.ds(turn_of(dve, dve_win, w, DENSE - 1) * FD, F)]
                    dve.wait_ge(dense_done, w + dense_n * h + 1)
                    nc.vector.tensor_tensor(a, a, bank[5][:, 0:F], ALU.add).then_inc(dense_acc, 1)

                def hop_turn(t, dense=False, last=False):
                    to = turn_of(dve, dve_turn, t + first_turn)
                    if not last:
                        after = turn_of(dve, dve_after, t + first_turn + 1)
                    sp_t = spans(dve, to)
                    for s in range(RING):
                        if s < RING - 1 or not last:
                            tn, sn = (to, s + 1) if s < RING - 1 else (after, 0)
                            one_hots(tn, sn, sp_t[s + 1])
                        dve.wait_ge(gathered[s], (t + hop_turns * h) * (16 * G) + 16 * G * (TURNS + 1))
                        accumulate((t + hop_turns * h) * RING + (SUPERS + s), to, s, sp_t[s], F)
                        stage(first_turn if last else after, s).then_inc(rows_free, 1)
                    if dense:
                        add_dense(t)

                one_hots(first_turn, 0, spans(dve, first_turn)[0])
                with dve.If(dense_t > 0):
                    with dve.If(hop_turns > dense_t):
                        with dve.Fori(0, dense_t) as t:
                            hop_turn(t, dense=True)
                    with dve.Else():
                        with dve.Fori(0, hop_turns - 1) as t:
                            hop_turn(t, dense=True)
                with dve.If(hop_turns > dense_t + 1):
                    with dve.Fori(dense_t, hop_turns - 1) as t:
                        hop_turn(t)
                with dve.If(hop_turns > dense_t):
                    hop_turn(hop_turns - 1, last=True)
                with dve.Else():
                    hop_turn(hop_turns - 1, dense=True, last=True)
                with dve.If(dense_n > dense_t):
                    with dve.Fori(dense_t, dense_n) as w:
                        add_dense(w)
                        hold(dve, dense_acc, w + dense_n * h + 2)
                hold(dve, acc_done, (hop_turns * (h + 1)) * RING + (SUPERS + 2))
                if h == 0:
                    nc.vector.tensor_tensor(agg3[:, :, 0:F], agg3[:, :, 0:F],
                                            inv[:, :].unsqueeze(2).to_broadcast([P, WINDOWS, F]),
                                            ALU.mult).then_inc(s_g, 1)
                    dve.wait_ge(s_g, 2)
            dve.wait_ge(s_x1, 32)

            def second_norm(j, nw):
                w0 = j * GROUP
                for i in range(nw):
                    xw = xs[:, bass.ds((w0 + i) * F, F)]
                    st = nc.vector.scalar_tensor_tensor(out=xw, in0=agg[:, bass.ds((w0 + i) * FD, F)],
                                                        scalar=dis[:, bass.ds(w0 + i, 1)], in1=xw,
                                                        op0=ALU.mult, op1=ALU.add)
                st.then_inc(b_y, 1)
                hold(dve, b_y, j + (GROUPS + 2))
                layer_norm(j, nw, j + GROUPS, True)
                dve.sem_inc(ln, 2)
                dve.sem_inc(s_res, 1)

            with dve.Fori(0, GROUPS - 1) as j:
                second_norm(j, GROUP)
            second_norm(GROUPS - 1, LAST)


_INS = ['x', 'src', 'dst', 'edge_attr_32', 'L0_gnn_We', 'L0_gnn_be', 'L0_gnn_W1', 'L0_gnn_b1',
        'L0_gnn_W2', 'L0_gnn_b2', 'L0_gnn_gamma', 'L0_gnn_beta']
_OUTS = [((12500, 96), 'float32')]


def kernel(**inputs):
    import numpy as _np
    import concourse.bacc as _bacc
    from concourse import mybir as _mybir
    from concourse.bass_utils import run_bass_kernel_spmd as _run

    nc = _bacc.Bacc("TRN2", target_bir_lowering=False, num_devices=1)
    arrays, args = {}, []
    for name in _INS:
        a = _np.ascontiguousarray(inputs[name])
        arrays[f"in_{name}_dram"] = a
        args.append(nc.dram_tensor(f"in_{name}_dram", a.shape, _mybir.dt.from_np(a.dtype), kind="ExternalInput").ap())
    for i, (shape, dtype) in enumerate(_OUTS):
        dt = _mybir.dt.from_np(_np.dtype(dtype))
        args.append(nc.dram_tensor(f"out_{i}_dram", shape, dt, kind="ExternalOutput").ap())
    gnn_kernel(nc, *args)
    r = _run(nc, [arrays], core_ids=[0])
    return r.results[0]["out_0_dram"]
```

```python
from contextlib import ExitStack

import concourse.bass as bass
from concourse import mybir

F32 = mybir.dt.float32
I32 = mybir.dt.int32
U32 = mybir.dt.uint32
BF16 = mybir.dt.bfloat16
F16 = mybir.dt.float16
ALU = mybir.AluOpType
ACT = mybir.ActivationFunctionType
AX_X = mybir.AxisListType.X

P = 128
EPS = 1e-5


def gnn_kernel(nc, x, src, dst, ea, We, be, W1, b1, W2, b2, gamma, beta, out):
    N, F = x.shape
    E, D = ea.shape
    WINDOWS = -(-N // P)
    TAIL = N - (WINDOWS - 1) * P
    G = 5
    SUPER = G * P
    SUPERS = E // SUPER
    RING = 5
    TURNS = SUPERS // RING
    SLOT = (0, 1, 0, 1, 2)
    ROWS = SUPERS // RING
    assert E % (SUPER * RING) == 0 and ROWS <= P and 4 * D == P and F * G <= 512
    FD = F + 1
    GROUP = 4
    GROUPS = -(-WINDOWS // GROUP)
    GN = GROUP * P
    NORM = 2 * GROUP
    NORMS = WINDOWS // NORM
    NLAST = WINDOWS - NORMS * NORM
    LAST = WINDOWS - (GROUPS - 1) * GROUP
    assert NLAST == LAST and NORMS % 2 == 0 and GROUPS == 2 * NORMS + 1
    BN = 500
    assert N % BN == 0 and GROUPS % 2 == 1

    DENSE = 31
    SUBN = 4
    SUBS = DENSE * P // SUBN
    SUBW = WINDOWS * SUBN
    HALF = SUBW // 2
    PER = 3
    LOWS = 1
    TV = PER * RING
    VISITS = PER * SUPERS
    CHUNKS = E // P
    PAIRS = -(-CHUNKS // 2)
    CG = -(-(SUBS + 1) // P)
    HOTS = 5
    DIV = 1024
    assert LOWS < PER and SUBW < 512 and WINDOWS % 2 == 0 and SUBS + TV <= DIV and TV % HOTS == 0 and VISITS - SUBS < PAIRS
    a_dram = nc.dram_tensor("counts_scratch", (P, 2, SUBS + TV, HALF), F32, kind="Internal").ap()
    cnt_dram = nc.dram_tensor("pairs_scratch", (CG * P,), F32, kind="Internal").ap()
    x1_dram = nc.dram_tensor("x1_scratch", (WINDOWS * P, F), F32, kind="Internal").ap()
    xb_dram = nc.dram_tensor("xb_scratch", (WINDOWS * P, F), F32, kind="Internal").ap()
    g_dram = [nc.dram_tensor(f"g{h}_scratch", (WINDOWS * P, F), F32, kind="Internal").ap() for h in range(2)]
    SPAN = 2 * RING + 2
    assert SPAN % 4 == 0
    span_dram = nc.dram_tensor("span_scratch", (TURNS, SPAN), I32, kind="Internal").ap()

    with ExitStack() as ctx:
        def sb(name, shape, dt=F32):
            return ctx.enter_context(nc.sbuf_tensor(name, shape, dt))

        def sem(name):
            return ctx.enter_context(nc.semaphore(name))

        bank = [ctx.enter_context(nc.psum_tensor(f"bank{i}", [P, 512], F32)) for i in range(5)]
        count_ps = ctx.enter_context(nc.psum_tensor("count_ps", [P, 3 * 512], F32))
        bank += [count_ps[:, i * 512:(i + 1) * 512] for i in range(3)]
        eaT_ps = bank[0]
        seg_ps = [bank[3], bank[4]]
        emb_ps = [bank[1], bank[2]]

        ident = sb("ident", [P, P])
        node_i = sb("node_i", [P, P], I32)
        node = sb("node", [P, P])
        base_i = sb("base_i", [P, WINDOWS], I32)
        base = sb("base", [P, WINDOWS])
        sub_base = sb("sub_base", [P, SUBS])
        key_i = sb("key_i", [P, SUBW], I32)
        zero_b = sb("zero_b", [P, P], BF16)
        pick = sb("pick", [P, P])
        ones = sb("ones", [P, P])
        thr_i = sb("thr_i", [P, CG], I32)
        thr = sb("thr", [P, CG])
        cnt_f = sb("cnt_f", [P, CG])
        cnt_g = sb("cnt_g", [P, CG])
        vis_i = sb("vis_i", [ROWS, TV + 2], I32)
        vis = sb("vis", [ROWS, TV + 2])
        spare_i = sb("spare_i", [ROWS, TV], I32)
        spare = sb("spare", [ROWS, TV])
        sub = sb("sub", [ROWS, TV + 2])
        sub_n = sb("sub_n", [ROWS, TV], I32)
        par_n = sb("par_n", [ROWS, TV], I32)
        fields = sb("fields", [ROWS, 8, TV])
        packed = sb("packed", [ROWS, 6, RING])
        words = sb("words", [ROWS, 6, RING], I32)
        tab_dve = sb("tab_dve", [ROWS, 12], I32)
        tab_pe = sb("tab_pe", [ROWS, 8], I32)
        tab_act = sb("tab_act", [ROWS, 8], I32)
        tab_sp = sb("tab_sp", [ROWS, 8], I32)
        nxt_i = sb("nxt_i", [ROWS, 1], I32)
        nxt = sb("nxt", [ROWS, 1])
        checks = sb("checks", [ROWS, 3])
        check2 = sb("check2", [ROWS, 2])
        dense_f = sb("dense_f", [P, 2])
        lim = sb("lim", [P, 1])
        okay = sb("okay", [P, 1])
        ctl_f = sb("ctl_f", [1, 9])
        ctl = sb("ctl", [1, 5], I32)
        eps = sb("eps", [P, 1])
        wide = sb("wide", [P, 4 * RING * SUPER])
        raw = {n: wide[0:ROWS, i * RING * SUPER:(i + 1) * RING * SUPER].bitcast(I32) for i, n in enumerate(("src", "dst"))}
        flt = {n: wide[0:ROWS, (2 + i) * RING * SUPER:(3 + i) * RING * SUPER] for i, n in enumerate(("src", "dst"))}
        h2T = wide[0:F, 0:WINDOWS * P]
        C2 = 2 * PAIRS
        src_c, dst_c = (wide[:, i * C2:(i + 1) * C2] for i in range(2))
        src_ci, dst_ci = src_c.bitcast(I32), dst_c.bitcast(I32)
        at = 2 * C2
        stage_a = wide[:, at:at + HOTS * SUBW].rearrange("p (s h c) -> p s h c", s=HOTS, h=2)
        at += HOTS * SUBW
        key_hot = wide[:, at:at + HOTS * SUBW].bitcast(BF16)
        at += HOTS * SUBW
        low_hot = wide[:, at:at + HOTS * P].bitcast(BF16)
        at += HOTS * P
        key_no = wide[:, at:at + SUBW // 2].bitcast(F16)
        assert at + SUBW // 2 <= 4 * RING * SUPER and HOTS * SUBW % 2 == 0
        blocks = [wide[:, h * (P // SUBN) * HALF:(h + 1) * (P // SUBN) * HALF].rearrange("p (n v) -> p n v", v=WINDOWS // 2) for h in range(2)]
        assert 2 * (P // SUBN) * HALF <= 4 * RING * SUPER
        src_all = sb("src_all", [P, SUPERS * G], U32)
        dst_all = sb("dst_all", [P, SUPERS * G])
        span_f = sb("span_f", [ROWS, RING, 2])
        span_n = sb("span_n", [ROWS, RING, 2], I32)
        span_w = sb("span_w", [ROWS, RING, 2], I32)
        span = sb("span", [1, TURNS * SPAN], I32)
        xs = sb("xs", [P, WINDOWS * F])
        agg = sb("agg", [P, WINDOWS * FD])
        dis = sb("dis", [P, WINDOWS])
        inv = sb("inv", [P, WINDOWS])
        deg = sb("deg", [P, WINDOWS])
        root = sb("root", [P, WINDOWS])
        be_all = sb("be_all", [P, F])
        We4 = sb("We4", [P, 4 * F])
        W1_sb = sb("W1_sb", [F, F])
        W2_sb = sb("W2_sb", [F, F])
        cols = sb("cols", [F, 4])
        idx = sb("idx", [P, RING * G], U32)
        rows = sb("rows", [P, RING, G * F])
        ea_sb = sb("ea_sb", [P, RING, G * D])
        eaT = sb("eaT", [P, 2 * P])
        msg = sb("msg", [P, 3, G * FD])
        hot = sb("hot", [P, 6, SUPER])
        flat = msg[:, :, :].rearrange("p s e -> p (s e)")
        hs = flat[:, 0:GROUP * F].rearrange("p (w f) -> p w f", f=F)
        hT = [flat[0:F, GROUP * F + i * GN:GROUP * F + (i + 1) * GN] for i in range(2)]
        hid = [hot[0:F, 0:2, :].rearrange("p s e -> p (s e)")[:, i * GN:(i + 1) * GN] for i in range(2)]
        yT = hT
        sub_i = hot[:, :, :].rearrange("p s e -> p (s e)")[:, 0:SUBS].bitcast(I32)
        stats = sb("stats", [F, N // BN, 6])
        mv = sb("mv", [F, 2])
        bn = sb("bn", [F, 4])
        bnt = sb("bnt", [F, 1])
        lst = sb("lst", [P, NORM, 6])
        lmv = sb("lmv", [P, NORM, 2])
        lroot = sb("lroot", [P, NORM])
        lrs = sb("lrs", [P, NORM])

        agg3 = agg[:, :].rearrange("p (w f) -> p w f", f=FD)
        xs3 = xs[:, :].rearrange("p (w f) -> p w f", f=F)
        msg3 = [msg[:, s, :].rearrange("p (g f) -> p g f", f=FD) for s in SLOT]
        hot3, second3 = ([hot[:, i + s, :].rearrange("p (g n) -> p g n", n=P) for s in SLOT] for i in (0, 3))
        last_dst = hot[:, :, :].rearrange("p s e -> p (s e)")
        before_sub = agg[:, 0:SUBS + 1]
        stats2 = stats[:, :, :].rearrange("p n s -> p (n s)")

        s_raw = sem("s_raw")
        s_x = sem("s_x")
        s_w = sem("s_w")
        s_wz = sem("s_wz")
        s_xz = sem("s_xz")
        s_iota = sem("s_iota")
        s_const = sem("s_const")
        s_constf = sem("s_constf")
        s_flt = sem("s_flt")
        s_span = sem("s_span")
        s_spand = sem("s_spand")
        s_xb = sem("s_xb")
        s_tab = sem("s_tab")
        s_zero = sem("s_zero")
        s_cut = sem("s_cut")
        s_key = sem("s_key")
        s_nxt = sem("s_nxt")
        s_chk = sem("s_chk")
        s_tot = sem("s_tot")
        s_ctl = sem("s_ctl")
        s_ctlf = sem("s_ctlf")
        s_cnt = sem("s_cnt")
        s_cntp = sem("s_cntp")
        s_cntd = sem("s_cntd")
        flat_turned = sem("flat_turned")
        flat_taken = sem("flat_taken")
        pair_hot = sem("pair_hot")
        s_vis = sem("s_vis")
        s_low = sem("s_low")
        low_square = sem("low_square")
        low_ready = sem("low_ready")
        visit_done = sem("visit_done")
        visit_copied = sem("visit_copied")
        stored = [sem(f"stored{i}") for i in range(HOTS)]
        block_in = [sem(f"block_in{h}") for h in range(2)]
        block_used = [sem(f"block_used{h}") for h in range(2)]
        dense_done = sem("dense_done")
        dense_acc = sem("dense_acc")
        s_x1 = sem("s_x1")
        x1_in = [sem(f"x1_in{i}") for i in range(2)]
        s_gc = sem("s_gc")
        idx_turned = sem("idx_turned")
        idx_taken = sem("idx_taken")
        held = sem("held")
        gathered = [sem(f"gathered{s}") for s in range(RING)]
        rows_free = sem("rows_free")
        ea_in = [sem(f"ea_in{s}") for s in range(RING)]
        ea_turned = sem("ea_turned")
        eaT_taken = sem("eaT_taken")
        embedded = sem("embedded")
        relu_done = sem("relu_done")
        hot_ready = sem("hot_ready")
        seg_done = sem("seg_done")
        acc_done = sem("acc_done")
        second_hot = sem("second_hot")
        second_seg = sem("second_seg")
        more_hot = sem("more_hot")
        more_seg = sem("more_seg")
        more_acc = sem("more_acc")
        m_h = sem("m_h")
        m_T = sem("m_T")
        m_Tc = sem("m_Tc")
        m_1 = sem("m_1")
        m_1a = sem("m_1a")
        m_2 = sem("m_2")
        m_2a = sem("m_2a")
        m_st = sem("m_st")
        s_bn = sem("s_bn")
        s_bna = sem("s_bna")
        s_deg = sem("s_deg")
        s_dega = sem("s_dega")
        b_a = sem("b_a")
        b_T = sem("b_T")
        b_y = sem("b_y")
        ln = sem("ln")
        ln_v = sem("ln_v")
        ln_r = sem("ln_r")
        s_scaled = sem("s_scaled")
        s_res = sem("s_res")
        s_out = sem("s_out")

        VIS = TV + 36

        block = ctx.enter_context(nc.Block())

        def hold(eng, semaphore, value):
            eng.wait_ge(semaphore, value)
            eng.sem_inc(held, 1)

        CH = 5

        def step_windows(tile, width, i, nw):
            return tile[:, bass.ds(i * (NORM * width), nw * width)].rearrange("p (w f) -> p w f", f=width)

        def nodes(t):
            return t.rearrange("(w p) f -> p w f", p=P)

        def spans(eng, t):
            _, v = nc.values_load_multi_w_load_instructions(
                span[0:1, bass.ds(t * SPAN, SPAN)], engines=[eng.engine], min_val=0, max_val=WINDOWS - 1,
                skip_runtime_bounds_check_because="destinations past the last node were clamped")
            return [(v[2 * i], v[2 * i + 1]) for i in range(RING + 1)]

        def first_span(eng, t):
            _, v = nc.values_load_multi_w_load_instructions(
                span[0:1, bass.ds(t * SPAN, 2)], engines=[eng.engine], min_val=0, max_val=WINDOWS - 1,
                skip_runtime_bounds_check_because="destinations past the last node were clamped")
            return v

        def table(eng, tab, t, lo, hi, most):
            _, v = nc.values_load_multi_w_load_instructions(
                bass.at_runtime_partition(tab[0:1, lo:hi], t), engines=[eng.engine], min_val=0, max_val=most,
                skip_runtime_bounds_check_because="the chip packed it from clamped fields")
            return v

        def windows_of(eng, registers, word):
            return [turn_of(eng, r, (word >> (7 * i)) & (P - 1), WINDOWS - 1) for i, r in enumerate(registers)]

        def control(eng):
            eng.wait_ge(s_ctl, 1)
            lim = [(0, TURNS - 2), (2, TURNS), (0, DENSE), (0, DENSE), (0, DENSE)]
            return [eng.value_load(ctl[0:1, i:i + 1], min_val=a, max_val=b) for i, (a, b) in enumerate(lim)]

        def turn_of(eng, register, turn, most=TURNS - 1):
            eng.reg_mov(register, turn)
            return eng.snap(register, min_val=0, max_val=most)

        @block.sync
        def _(sp):
            for n, t in (("src", src), ("dst", dst)):
                sp.dma_start(raw[n], t.rearrange("(r e) -> r e", r=ROWS)).then_inc(s_raw, 16)
            sp.dma_start(nxt_i[0:ROWS - 1, :], dst[RING * SUPER:].rearrange("(r e) -> r e", e=RING * SUPER)[:, 0:1],
                         allow_slow_non_contiguous=True).then_inc(s_nxt, 16)
            sp.dma_start(nxt_i[ROWS - 1:ROWS, :], dst[E - 1:E].rearrange("(a e) -> a e", a=1)).then_inc(s_nxt, 16)
            sp.wait_ge(s_xz, 1)
            sp.dma_start(xs3[:, 0:WINDOWS - 1, :], nodes(x[0:N - TAIL, :])).then_inc(s_x, 16)
            sp.dma_start(xs3[0:TAIL, WINDOWS - 1, :], x[N - TAIL:N, :]).then_inc(s_x, 16)
            sp.dma_start(be_all[:, :], be.rearrange("(a f) -> a f", a=1).to_broadcast([P, F])).then_inc(s_x, 16)
            sp.wait_ge(s_wz, 1)
            for j in range(4):
                sp.dma_start(We4[j * D:(j + 1) * D, j * F:(j + 1) * F], We).then_inc(s_w, 16)
            sp.dma_start(W1_sb[:, :], W1).then_inc(s_w, 16)
            sp.dma_start(W2_sb[:, :], W2).then_inc(s_w, 16)
            for j, t in enumerate((b1, b2, gamma, beta)):
                sp.dma_start(cols[:, j:j + 1], t.rearrange("(f a) -> f a", a=1)).then_inc(s_w, 16)
            sp.wait_ge(s_span, 5)
            own = span_w[:, :, :].rearrange("r k s -> r (k s)")
            sp.dma_start(span_dram[:, 0:2 * RING], own).then_inc(s_spand, 16)
            sp.dma_start(span_dram[0:TURNS - 1, 2 * RING:SPAN], own[1:ROWS, 0:2]).then_inc(s_spand, 16)
            sp.dma_start(span_dram[TURNS - 1:TURNS, 2 * RING:SPAN], own[0:1, 0:2]).then_inc(s_spand, 16)
            sp.wait_ge(s_spand, 48)
            sp.dma_start(span[:, :], span_dram.rearrange("(a r) s -> a (r s)", a=1)).then_inc(s_spand, 16)
            sp.wait_ge(s_xb, 1)
            sp.dma_start(nodes(xb_dram), agg3[:, :, 0:F]).then_inc(s_tab, 16)
            sp.wait_ge(s_cnt, CG + 1)
            sp.dma_start(cnt_dram.rearrange("(p c) -> p c", p=P), cnt_g[:, :]).then_inc(s_cntd, 16)
            sp.wait_ge(s_cntd, 16)
            sp.wait_ge(s_tab, 16)
            sp.dma_start(before_sub, cnt_dram[0:SUBS + 1].rearrange("(a n) -> a n", a=1).to_broadcast([P, SUBS + 1])
                         ).then_inc(s_cntd, 16)
            ea_v = ea.rearrange("(k p g) d -> k p (g d)", p=P, g=G)
            sp_to = sp.alloc_register("sp_to")

            def load_ea(t, s):
                return sp.dma_start(ea_sb[:, s, :], ea_v[bass.ds(t * RING + s, 1), :, :].rearrange("k p e -> (k p) e")
                                    ).then_inc(ea_in[s], 16)

            def store_counts(t, s, i, to):
                slot = (PER * s + i) % HOTS
                hold(sp, visit_copied, t * TV + (PER * s + i + 2))
                with sp.If(to < SUBS):
                    at = turn_of(sp, sp_to, to, SUBS + TV - 1)
                    sp.dma_start(a_dram[:, :, bass.ds(at, 1), :].rearrange("p h a c -> p h (a c)"),
                                 stage_a[:, slot, :, :]).then_inc(stored[slot], 16)
                with sp.Else():
                    sp.dma_start(a_dram[0:1, 0, SUBS + PER * s + i, :], stage_a[0:1, slot, 0, :]).then_inc(stored[slot], 16)

            def turn(t, last):
                row = table(sp, tab_sp, t, 0, RING, DIV ** 3 - 1)
                for s in range(RING):
                    for i in range(PER):
                        store_counts(t, s, i, (row[s] >> (10 * i)) & (DIV - 1))
                    if not last:
                        sp.wait_ge(ea_turned, t * RING + (RING + s + 1))
                        load_ea(t + 1, s)

            for s in range(RING):
                load_ea(0, s)
            sp.wait_ge(s_vis, VIS)
            with sp.Fori(0, TURNS - 1) as t:
                turn(t, False)
            turn(TURNS - 1, True)
            def store_norm(i, nw):
                hold(sp, ln, i * CH + (CH + 1))
                sp.dma_start(nodes(g_dram[0])[:, bass.ds(i * NORM, nw), :], step_windows(agg, FD, i, nw)[:, :, 0:F]).then_inc(s_tab, 16)
                sp.dma_start(nodes(x1_dram)[:, bass.ds(i * NORM, nw), :], step_windows(xs, F, i, nw)).then_inc(s_x1, 16)

            with sp.Fori(0, NORMS) as i:
                store_norm(i, NORM)
            store_norm(NORMS, NLAST)
            sp.wait_ge(s_ctl, 1)
            dense_n = sp.value_load(ctl[0:1, 2:3], min_val=0, max_val=DENSE)
            for i in range(HOTS):
                sp.wait_ge(stored[i], 16 * (TURNS * (TV // HOTS) + 1))
            for h in range(2):
                if h == 1:
                    def store_sums(i, nw):
                        hold(sp, s_scaled, i + 1)
                        sp.dma_start(nodes(g_dram[1])[:, bass.ds(i * NORM, nw), :], step_windows(agg, FD, i, nw)[:, :, 0:F]).then_inc(s_tab, 16)

                    with sp.Fori(0, NORMS) as i:
                        store_sums(i, NORM)
                    store_sums(NORMS, NLAST)
                with sp.If(dense_n > 0):
                    with sp.Fori(0, dense_n) as w:
                        for i in range(2):
                            hold(sp, block_used[i], w + dense_n * h + 1)
                            sp.dma_start(blocks[i].rearrange("p n v -> p (n v)"),
                                         a_dram[:, i, bass.ds(w * (P // SUBN), P // SUBN), :].rearrange("p u c -> p (u c)")
                                         ).then_inc(block_in[i], 16)
            hold(sp, dense_acc, dense_n * 2 + 1)
            sp.wait_ge(s_gc, 2)
            def load_x1(i, b, nw):
                hold(sp, x1_in[b], i * 16 + 16)
                sp.dma_start(step_windows(xs, F, i * 2 + b, nw), nodes(x1_dram)[:, bass.ds(i * (2 * NORM) + b * NORM, nw), :]).then_inc(x1_in[b], 16)

            with sp.Fori(0, NORMS // 2) as i:
                for b in range(2):
                    load_x1(i, b, NORM)
            load_x1(NORMS // 2, 0, NLAST)
            sp.wait_ge(s_out, 16 * (NORMS + 2))

        @block.gpsimd
        def _(pool):
            nc.gpsimd.memset(xs3[:, WINDOWS - 1, :], 0.0).then_inc(s_xz, 1)
            nc.gpsimd.memset(We4[:, :], 0.0).then_inc(s_wz, 1)
            nc.gpsimd.memset(ident[:, :], 0.0).then_inc(s_iota, 1)
            nc.gpsimd.memset(eps[:, :], EPS).then_inc(s_const, 1)
            nc.gpsimd.iota(node_i[:, :], pattern=[[1, P]], base=0, channel_multiplier=0).then_inc(s_const, 1)
            nc.gpsimd.iota(base_i[:, :], pattern=[[P, WINDOWS]], base=0, channel_multiplier=0).then_inc(s_const, 1)
            nc.gpsimd.iota(sub_i[:, :], pattern=[[1024, SUBS]], base=0, channel_multiplier=0).then_inc(s_const, 1)
            nc.gpsimd.iota(thr_i[:, :], pattern=[[SUBN, CG]], base=0, channel_multiplier=SUBN * CG).then_inc(s_const, 1)
            nc.gpsimd.iota(key_i[:, :], pattern=[[1, SUBW]], base=0, channel_multiplier=0).then_inc(s_const, 1)
            nc.gpsimd.memset(ones[:, :], 1.0).then_inc(s_const, 1)
            nc.gpsimd.memset(pick[:, :], 0.0).then_inc(s_iota, 1)
            nc.gpsimd.memset(zero_b[:, :], 0.0).then_inc(s_const, 1)
            nc.gpsimd.iota(vis_i[:, :], pattern=[[1, TV + 2]], base=-1, channel_multiplier=TV).then_inc(s_const, 1)
            nc.gpsimd.iota(spare_i[:, :], pattern=[[1, TV]], base=SUBS, channel_multiplier=0).then_inc(s_const, 1)
            pool.wait_ge(s_iota, 2)
            nc.gpsimd.affine_select(out=pick[:, :], in_=pick[:, :], compare_op=ALU.not_equal, fill=1.0, base=-(P - 1),
                                    pattern=[[0, P]], channel_multiplier=1).then_inc(s_const, 1)
            nc.gpsimd.affine_select(out=ident[:, :], in_=ident[:, :], compare_op=ALU.not_equal, fill=1.0, base=0,
                                    pattern=[[-1, P]], channel_multiplier=1).then_inc(s_const, 1)
            pool.wait_ge(s_vis, 1)
            nc.gpsimd.memset(agg[:, :], 0.0).then_inc(s_zero, 1)
            pool.wait_ge(idx_taken, 2 * RING * G + 1)
            for p in range(3):
                if p == 1:
                    pool.wait_ge(s_ctl, 1)
                    hop_turns = pool.value_load(ctl[0:1, 1:2], min_val=2, max_val=TURNS)
                table = [xb_dram, *g_dram][p]
                pool.wait_ge(s_tab, 16 * (1 + p * (NORMS + 1)))
                before = 0 if p == 0 else hop_turns * ((p - 1) * RING) + SUPERS
                with pool.Fori(0, TURNS if p == 0 else hop_turns) as t:
                    for s in range(RING):
                        hold(pool, rows_free, t * RING + before + (s + 1))
                        for g in range(G):
                            pool.indirect_dma_start(
                                rows[:, s, g * F:(g + 1) * F], None, table,
                                bass.IndirectOffsetOnAxis(ap=idx[:, s * G + g:s * G + g + 1], axis=0),
                            ).then_inc(gathered[s], 16)

        @block.tensor
        def _(pe):
            pe.wait_ge(s_const, 12)
            pe.wait_ge(s_flt, 2)
            for b in range(RING):
                for g in range(G):
                    if b:
                        pe.wait_ge(idx_taken, 2 * ((b - 1) * G + g + 1))
                    for i, n in enumerate(("src", "dst")):
                        v = flt[n][:, b * SUPER:(b + 1) * SUPER].rearrange("r (q g) -> r g q", g=G)[:, g, :]
                        nc.tensor.transpose(bank[g][:, i * P:i * P + ROWS], v, ident[0:ROWS, 0:ROWS]).then_inc(idx_turned, 1)

            for c in range(RING * G):
                if c >= 3:
                    pe.wait_ge(flat_taken, 2 * (c - 2))
                for i, n in enumerate(("src", "dst")):
                    nc.tensor.transpose(bank[5 + c % 3][:, i * P:i * P + ROWS], flt[n][:, c * P:(c + 1) * P],
                                        ident[0:ROWS, 0:ROWS]).then_inc(flat_turned, 1)
            pe.wait_ge(s_chk, 6)
            pe.wait_ge(idx_taken, 2 * RING * G)
            nc.tensor.matmul(bank[0][:, 0:1], ones[0:ROWS, :], check2[:, 0:1], start=True, stop=True).then_inc(s_tot, 1)
            pe.wait_ge(s_key, 1)
            for i in range(4):
                n = min(512, PAIRS - 1 - i * 512)
                v = last_dst[:, 0:2 * (PAIRS - 1)].rearrange("p (j b) -> p j b", b=2)[:, i * 512:i * 512 + n, 1]
                nc.tensor.matmul(bank[1 + i][:, 0:n], pick[:, :], v, start=True, stop=True).then_inc(s_cntp, 1)

            pe_second, pe_more = (pe.alloc_register(f"pe_{n}") for n in ("second", "more"))
            for r in (pe_second, pe_more):
                pe.reg_mov(r, 0)

            def segment(k, s, span_s, rhs, width, between=None):
                def products(rows_of, at, between=None):
                    for g in range(G):
                        if g == 2 and between is not None:
                            between()
                        mm = nc.tensor.matmul(seg_ps[s % 2][:, at:at + width], rows_of[s][:, g, :], rhs(g),
                                              start=(g == 0), stop=(g == G - 1))
                    return mm
                pe.wait_ge(hot_ready, k + 1)
                pe.wait_ge(acc_done, k + (2 if s == 0 else 1))
                products(hot3, 0, between).then_inc(seg_done, 1)
                first, last = span_s
                with pe.If(last > first):
                    pe.wait_ge(second_hot, pe.snap(pe_second) + 1)
                    products(second3, P).then_inc(second_seg, 1)
                    pe.reg_add(pe_second, pe_second, 1)
                    with pe.If(last > first + 1):
                        with pe.Fori(first + 1, last):
                            pe.wait_ge(more_hot, pe.snap(pe_more) + 1)
                            products(hot3, 0).then_inc(more_seg, 1)
                            pe.reg_add(pe_more, pe_more, 1)
                            hold(pe, more_acc, pe.snap(pe_more) + 1)

            def turn_ea(t, s):
                k = t * RING + s
                pe.wait_ge(ea_in[s], t * 16 + 16)
                pe.wait_ge(eaT_taken, k + 1)
                nc.tensor.transpose(eaT_ps[:, 0:P], ea_sb[:, s, 0:P], ident[:, :])
                nc.tensor.transpose(eaT_ps[0:D, P:2 * P], ea_sb[:, s, P:P + D], ident[:, :]).then_inc(ea_turned, 1)

            def embed(t, s, part):
                k = t * RING + s
                if part == 0:
                    pe.wait_ge(eaT_taken, k + 2)
                    pe.wait_ge(rows_free, k + (RING if s == 0 else RING - 1))
                    nc.tensor.matmul(emb_ps[s % 2][:, 0:4 * F], eaT[:, 0:P], We4[:, :], start=True, stop=True)
                else:
                    nc.tensor.matmul(emb_ps[s % 2][:, 4 * F:5 * F], eaT[0:D, P:2 * P], We4[0:D, 0:F],
                                     start=True, stop=True).then_inc(embedded, 1)

            pe.wait_ge(s_w, 160)
            pe.wait_ge(s_spand, 64)
            pe.wait_ge(s_cnt, CG)
            pe.wait_ge(s_low, 1)
            nc.tensor.matmul(bank[3][:, 0:1], ones[0:ROWS, :], check2[:, 1:2], start=True, stop=True).then_inc(s_tot, 1)
            pe.wait_ge(s_vis, VIS)
            turn_ea(0, 0)
            embed(0, 0, 0)
            embed(0, 0, 1)
            turn_ea(0, 1)

            def visit(t, s, i, code):
                v = t * TV + (PER * s + i)
                slot = (PER * s + i) % HOTS
                to = turn_of(pe, pe_to, (code & 1) * 512, 512)
                opened = turn_of(pe, pe_open, ((code >> 1) & 3) * 512 + 511, 1024 + 511)
                pe.wait_ge(visit_copied, v + 1)
                nc.tensor.matmul(count_ps[:, bass.ds(opened, 1)], zero_b[:, :], zero_b[:, 0:1],
                                 start=True, stop=False, skip_group_check=True)
                if i >= PER - LOWS:
                    pe.wait_ge(low_ready, t * (LOWS * RING) + (LOWS * (s + 1) - PER + i + 1))
                pe.wait_ge(pair_hot, v + 1)
                for c in range(2):
                    at = slot * 2 + c
                    mm = nc.tensor.matmul(count_ps[:, bass.ds(to, SUBW)], low_hot[:, at * P:(at + 1) * P],
                                          key_hot[:, at * SUBW:(at + 1) * SUBW], start=False, stop=(c == 1), skip_group_check=True)
                mm.then_inc(visit_done, 1)

            pe_windows = [[pe.alloc_register(f"pe_{n}{s}") for n in ("first", "last")] for s in range(RING)]
            pe_to = pe.alloc_register("pe_to")
            pe_open = pe.alloc_register("pe_open")

            def turn(t, last):
                row = table(pe, tab_pe, t, 0, RING, 8 ** PER * P * P - 1)
                for s in range(RING):
                    codes, span_s = row[s] >> 14, windows_of(pe, pe_windows[s], row[s])
                    following = [(t + (s + n) // RING, (s + n) % RING) for n in range(3)]
                    visit(t, s, 0, codes & 7)
                    if s < RING - 1 or not last:
                        embed(*following[1], 0)
                    visit(t, s, 1, (codes >> 3) & 7)
                    if s < RING - 1 or not last:
                        embed(*following[1], 1)
                    pe.wait_ge(relu_done, t * RING + s + 1)
                    segment(t * RING + s, s, span_s, lambda g: msg3[s][:, g, :], FD,
                            between=lambda: visit(t, s, 2, (codes >> 6) & 7))
                    if s < RING - 2 or not last:
                        turn_ea(*following[2])

            with pe.Fori(0, TURNS - 1) as t:
                turn(t, False)
            turn(TURNS - 1, True)

            def turn_h(j, nw):
                pe.wait_ge(m_h, j + 1)
                pe.wait_ge(m_Tc, j + 1)
                for i in range(nw):
                    tr = nc.tensor.transpose(bank[4][0:F, i * P:(i + 1) * P], hs[:, i, :], ident[:, :])
                tr.then_inc(m_T, 1)

            def first_product(j, b, nw):
                pe.wait_ge(m_Tc, j + 2)
                pe.wait_ge(m_1a, j + 1)
                nc.tensor.matmul(bank[5][0:F, 0:nw * P], W1_sb[:, :], hT[b][:, 0:nw * P], start=True, stop=True).then_inc(m_1, 1)

            def second_product(j, b, nw):
                pe.wait_ge(m_1a, j + 2)
                pe.wait_ge(m_2a, j + 1)
                nc.tensor.matmul(bank[6][0:F, 0:nw * P], W2_sb[:, :], hid[b][:, 0:nw * P], start=True, stop=True).then_inc(m_2, 1)

            turn_h(0, GROUP)
            turn_h(1, GROUP)
            first_product(0, 0, GROUP)
            with pe.Fori(0, NORMS - 1) as i:
                for b in range(2):
                    turn_h(i * 2 + (b + 2), GROUP)
                    first_product(i * 2 + (b + 1), 1 - b, GROUP)
                    second_product(i * 2 + b, b, GROUP)
            turn_h(GROUPS - 1, LAST)
            first_product(GROUPS - 2, 1, GROUP)
            second_product(GROUPS - 3, 0, GROUP)
            first_product(GROUPS - 1, 0, LAST)
            second_product(GROUPS - 2, 1, GROUP)
            second_product(GROUPS - 1, 0, LAST)

            def back(j, b, nw):
                pe.wait_ge(b_a, j + 1)
                pe.wait_ge(b_y, j + 1)
                for i in range(nw):
                    tr = nc.tensor.transpose(bank[4 + b][:, i * F:(i + 1) * F], yT[b][:, i * P:(i + 1) * P], ident[0:F, 0:F])
                tr.then_inc(b_T, 1)

            with pe.Fori(0, NORMS) as i:
                for b in range(2):
                    back(i * 2 + b, b, GROUP)
            back(GROUPS - 1, 0, LAST)

            first_turn, hop_turns, dense_n, dense_1, dense_2 = control(pe)
            pe_win = pe.alloc_register("pe_win")
            pe_turn = pe.alloc_register("pe_turn")
            hold(pe, s_cut, 1)
            for h in range(2):
                def dense_part(w, lo, hi):
                    for v in range(lo, hi):
                        half, i = divmod(v, WINDOWS // 2)
                        if v == 0:
                            pe.wait_ge(dense_acc, w + dense_n * h + 1)
                        if i == 0:
                            pe.wait_ge(block_in[half], (w + dense_n * h) * 16 + 16)
                        mm = nc.tensor.matmul(bank[5][:, 0:F], blocks[half][:, :, i],
                                              xs3[:, v, :], start=(v == 0), stop=(v == WINDOWS - 1))
                        if i == WINDOWS // 2 - 1:
                            mm.then_inc(block_used[half], 1)
                    if hi == WINDOWS:
                        nc.tensor.matmul(bank[5][:, 511:512], zero_b[:, :], zero_b[:, 0:1], start=False, stop=True,
                                         skip_group_check=True).then_inc(dense_done, 1)

                def hop_turn(t, dense=None):
                    sp_t = spans(pe, turn_of(pe, pe_turn, t + first_turn))
                    for s in range(RING):
                        if dense is not None:
                            w, lo, hi = dense
                            n = -(-(hi - lo) // RING)
                            dense_part(w, min(lo + n * s, hi), min(lo + n * (s + 1), hi))
                        pe.wait_ge(gathered[s], (t + hop_turns * h) * (16 * G) + 16 * G * (TURNS + 1))
                        segment((t + hop_turns * h) * RING + (SUPERS + s), s, sp_t[s], lambda g: rows[:, s, g * F:(g + 1) * F], F)

                pe.wait_ge(s_gc, h + 1)
                with pe.If(dense_1 > 0):
                    with pe.Fori(0, dense_1) as t:
                        hop_turn(t, (t, 0, WINDOWS))
                with pe.If(dense_2 > 0):
                    with pe.Fori(0, dense_2) as i:
                        for half in range(2):
                            hop_turn(dense_1 + i * 2 + half, (dense_1 + i, half * (WINDOWS // 2), (half + 1) * (WINDOWS // 2)))
                with pe.If(hop_turns > dense_1 + dense_2 * 2):
                    with pe.Fori(dense_1 + dense_2 * 2, hop_turns) as t:
                        hop_turn(t)
                with pe.If(dense_n > dense_1 + dense_2):
                    with pe.Fori(dense_1 + dense_2, dense_n) as w:
                        dense_part(w, 0, WINDOWS)

        @block.scalar
        def _(act):
            def take(t, s):
                k = t * RING + s
                act.wait_ge(embedded, k + 1)
                act.wait_ge(ea_turned, k + RING + 1)
                nc.scalar.copy(eaT[:, 0:P], eaT_ps[:, 0:P])
                nc.scalar.copy(eaT[0:D, P:2 * P], eaT_ps[0:D, P:2 * P]).then_inc(eaT_taken, 1)

            for c in range(RING * G):
                act.wait_ge(flat_turned, 2 * (c + 1))
                if c == 0:
                    act.wait_ge(s_flt, 2)
                for i, v in enumerate((src_ci, dst_ci)):
                    to = v[:, 0:CHUNKS].rearrange("q (r c) -> q c r", c=RING * G)[:, c, :]
                    nc.scalar.copy(to, bank[5 + c % 3][:, i * P:i * P + ROWS]).then_inc(flat_taken, 1)
            act.sem_inc(eaT_taken, 1)
            act.sem_inc(visit_copied, 1)
            for i in range(HOTS):
                act.sem_inc(stored[i], 16)
            act.sem_inc(m_1a, 1)
            act.sem_inc(m_2a, 1)
            take(0, 0)

            act_from, act_sub, act_chunk, act_word = (act.alloc_register(f"act_{n}") for n in ("from", "sub", "chunk", "word"))

            def low_rows(t, s, i, word):
                v, n, slot = t * TV + (PER * s + i), t * (LOWS * RING) + (LOWS * (s + 1) - PER + i), (PER * s + i) % HOTS
                w = turn_of(act, act_sub, (word >> (10 * i)) & (DIV - 1), SUBS - 1)
                chunk = turn_of(act, act_chunk, (v - w) * 2, 2 * (PAIRS - 1))
                act.wait_ge(visit_done, v + 1)
                for c in range(2):
                    at = slot * 2 + c
                    sq = nc.scalar.activation(low_hot[:, at * P:(at + 1) * P], node[:, :], ACT.Square, bias=src_c[:, bass.ds(chunk + c, 1)])
                sq.then_inc(low_square, 1)
                act.wait_ge(low_square, n + 1)
                both = low_hot[:, 2 * slot * P:2 * (slot + 1) * P]
                nc.scalar.activation(both, both, ACT.Relu, bias=ones[:, 0:1], scale=-1.0).then_inc(low_ready, 1)

            def take_counts(t, s, i, par):
                v = t * TV + (PER * s + i)
                before, slot = divmod(PER * s + i, HOTS)
                hold(act, stored[slot], t * (16 * (TV // HOTS)) + 16 * (before + 1))
                act.wait_ge(visit_done, v + (HOTS + 1))
                at = turn_of(act, act_from, par * 512, 512)
                nc.scalar.copy(stage_a[:, slot, :, :].rearrange("p h (d v) -> p h d v", d=SUBN),
                               count_ps[:, bass.ds(at, SUBW)].rearrange("p (d h v) -> p h d v", d=SUBN, h=2)).then_inc(visit_copied, 1)

            def turn(t, last):
                row = [act.snap(act_word), *table(act, tab_act, t, 1, RING, DIV ** 3 - 1)]
                for s in range(RING):
                    take_counts(t, s, 0, row[s] & 1)
                    act.wait_ge(rows_free, t * RING + (RING + s + 1))
                    nc.scalar.activation(msg3[s][:, :, 0:F], msg3[s][:, :, 0:F], ACT.Relu).then_inc(relu_done, 1)
                    if s < RING - 1:
                        following, word = (t, s + 1), row[s + 1]
                    elif not last:
                        act.reg_mov(act_word, table(act, tab_act, t + 1, 0, 1, DIV ** 3 - 1)[0])
                        following, word = (t + 1, 0), act.snap(act_word)
                    for i in range(1, PER):
                        take_counts(t, s, i, (row[s] >> (10 * i)) & 1)
                    if s < RING - 2 or not last:
                        take(t + (s + 2) // RING, (s + 2) % RING)
                    if s < RING - 1 or not last:
                        for i in range(PER - LOWS, PER):
                            low_rows(*following, i, word)

            act.wait_ge(s_vis, VIS)
            word = table(act, tab_act, 0, 0, 1, DIV ** 3 - 1)[0]
            act.reg_mov(act_word, word)
            for i in range(PER - LOWS, PER):
                low_rows(0, 0, i, word)
            take(0, 1)
            with act.Fori(0, TURNS - 1) as t:
                turn(t, False)
            turn(TURNS - 1, True)

            act.wait_ge(s_deg, 1)
            nc.scalar.activation(root[:, :], deg[:, :], ACT.Sqrt).then_inc(s_dega, 1)

            def first_out(j, b, nw):
                act.wait_ge(m_1, j + 3)
                act.wait_ge(m_2, j + 1)
                nc.scalar.activation(hid[b][:, 0:nw * P], bank[5][0:F, 0:nw * P], ACT.Relu, bias=cols[:, 0:1]).then_inc(m_1a, 1)

            def second_out(j, nw):
                act.wait_ge(m_2, j + 3)
                nc.scalar.activation(h2T[:, bass.ds(j * GN, nw * P)], bank[6][0:F, 0:nw * P], ACT.Identity, bias=cols[:, 1:2]).then_inc(m_2a, 1)

            for i in range(HOTS):
                act.wait_ge(stored[i], 16 * (TURNS * (TV // HOTS) + 1))
            act.sem_inc(m_2, 2)
            act.wait_ge(s_w, 160)
            first_out(0, 0, GROUP)
            with act.Fori(0, NORMS - 1) as i:
                for b in range(2):
                    first_out(i * 2 + (b + 1), 1 - b, GROUP)
                    second_out(i * 2 + b, GROUP)
            first_out(GROUPS - 2, 1, GROUP)
            second_out(GROUPS - 3, GROUP)
            first_out(GROUPS - 1, 0, LAST)
            second_out(GROUPS - 2, GROUP)
            second_out(GROUPS - 1, LAST)

            act.wait_ge(s_bn, 1)
            nc.scalar.activation(bn[:, 0:1], mv[:, 1:2], ACT.Sqrt, bias=eps[0:F, :]).then_inc(s_bna, 1)
            act.sem_inc(b_T, 2)
            act.wait_ge(s_bn, 5)

            def scale(j, b, nw):
                c = nw * P
                act.wait_ge(b_T, j + 1)
                nc.scalar.activation(yT[b][:, 0:c], h2T[:, bass.ds(j * GN, c)], ACT.Relu, bias=bn[:, 3:4], scale=bn[:, 2:3]).then_inc(b_a, 1)

            def ln_root(n):
                act.wait_ge(ln_v, n + 1)
                nc.scalar.activation(lroot[:, :], lmv[:, :, 1], ACT.Sqrt, bias=eps[:, :]).then_inc(ln_r, 1)

            for b in range(2):
                scale(b, b, GROUP)
            with act.Fori(0, NORMS - 1) as i:
                ln_root(i)
                for b in range(2):
                    scale(i * 2 + (b + 2), b, GROUP)
            ln_root(NORMS - 1)
            scale(GROUPS - 1, 0, LAST)
            ln_root(NORMS)

            def store_out(i, w, nw, rows_of=P):
                hold(act, s_res, i + 1)
                if rows_of == P:
                    act.dma_start(nodes(out[0:N - TAIL, :])[:, bass.ds(w, nw), :], xs[:, bass.ds(w * F, nw * F)].rearrange("p (w f) -> p w f", f=F)).then_inc(s_out, 16)
                else:
                    act.dma_start(out[N - rows_of:N, :], xs3[0:rows_of, w, :]).then_inc(s_out, 16)

            with act.Fori(0, NORMS) as i:
                ln_root(i + (NORMS + 1))
                store_out(i, i * NORM, NORM)
            ln_root(2 * NORMS + 1)
            store_out(NORMS, NORMS * NORM, NLAST - 1)
            store_out(NORMS, WINDOWS - 1, 1, TAIL)

        @block.vector
        def _(dve):
            dve.sem_inc(rows_free, RING)
            dve.sem_inc(visit_done, HOTS)
            dve.sem_inc(block_used[0], 1)
            dve.sem_inc(block_used[1], 1)
            dve.sem_inc(dense_acc, 1)
            dve.sem_inc(ea_turned, RING)
            dve.sem_inc(embedded, 1)
            dve.sem_inc(acc_done, 2)
            dve.sem_inc(more_acc, 1)
            dve.sem_inc(m_Tc, 1)
            dve.sem_inc(b_y, 2)
            for i in range(2):
                dve.sem_inc(x1_in[i], 16)
            nc.vector.memset(msg[:, :, :], 1.0).then_inc(s_constf, 1)
            nc.vector.memset(lmv[:, :, :], 1.0).then_inc(s_constf, 1)
            dve.wait_ge(s_raw, 32)
            for n in ("dst", "src"):
                nc.vector.tensor_copy(flt[n], raw[n]).then_inc(s_flt, 1)
            dve.wait_ge(s_flt, 1)
            d3 = flt["dst"].rearrange("r (k e) -> r k e", e=SUPER)
            nc.vector.tensor_reduce(span_f[:, :, 0], d3, AX_X, ALU.min).then_inc(s_span, 1)
            nc.vector.tensor_reduce(span_f[:, :, 1], d3, AX_X, ALU.max).then_inc(s_span, 1)
            dve.wait_ge(s_span, 2)
            nc.vector.tensor_scalar(span_f[:, :, :], span_f[:, :, :], float(N - 1), None, ALU.min).then_inc(s_span, 1)
            dve.wait_ge(s_span, 3)
            nc.vector.tensor_copy(span_n[:, :, :], span_f[:, :, :]).then_inc(s_span, 1)
            dve.wait_ge(s_span, 4)
            nc.vector.tensor_scalar(span_w[:, :, :], span_n[:, :, :], 7, None, ALU.arith_shift_right).then_inc(s_span, 1)
            d = flt["dst"]
            W = RING * SUPER
            dve.wait_ge(s_nxt, 32)
            nc.vector.tensor_copy(nxt[:, :], nxt_i[:, :]).then_inc(s_chk, 1)
            dve.wait_ge(s_flt, 2)
            nc.vector.tensor_tensor(agg[0:ROWS, 0:W - 1], d[:, 0:W - 1], d[:, 1:W], ALU.is_gt).then_inc(s_chk, 1)
            dve.wait_ge(s_chk, 2)
            nc.vector.tensor_reduce(checks[:, 0:1], agg[0:ROWS, 0:W - 1], AX_X, ALU.max).then_inc(s_chk, 1)
            nc.vector.tensor_tensor(checks[:, 1:2], d[:, W - 1:W], nxt[:, :], ALU.is_gt).then_inc(s_chk, 1)
            nc.vector.tensor_reduce(checks[:, 2:3], span_f[:, :, 1], AX_X, ALU.max).then_inc(s_chk, 1)
            dve.wait_ge(s_chk, 5)
            nc.vector.tensor_tensor(check2[:, 0:1], checks[:, 0:1], checks[:, 1:2], ALU.add).then_inc(s_chk, 1)
            dve.wait_ge(s_const, 12)
            nc.vector.tensor_copy(node[:, :], node_i[:, :]).then_inc(s_constf, 1)
            nc.vector.tensor_copy(base[:, :], base_i[:, :]).then_inc(s_constf, 1)
            nc.vector.tensor_copy(thr[:, :], thr_i[:, :]).then_inc(s_constf, 1)
            nc.vector.tensor_copy(sub_base[:, :], sub_i[:, :]).then_inc(s_constf, 1)
            nc.vector.tensor_copy(vis[:, :], vis_i[:, :]).then_inc(s_constf, 1)
            nc.vector.tensor_copy(spare[:, :], spare_i[:, :]).then_inc(s_constf, 1)
            srcv = src_all[:, :].rearrange("q (r c) -> q c r", c=RING * G)
            dstv = dst_all[:, :].rearrange("q (r c) -> q c r", c=RING * G)
            for b in range(RING):
                for g in range(G):
                    for i, v in enumerate((srcv, dstv)):
                        dve.wait_ge(idx_turned, 2 * (b * G + g + 1))
                        nc.vector.tensor_copy(v[:, b * G + g, :],
                                              bank[g][:, i * P:i * P + ROWS]).then_inc(idx_taken, 1)
            dve.wait_ge(idx_taken, 2 * RING * G)
            nc.vector.tensor_copy(idx[:, :], src_all[:, 0:RING * G]).then_inc(idx_taken, 1)
            dve.wait_ge(s_x, 48)
            nc.vector.tensor_tensor(agg3[:, :, 0:F], xs3, be_all[:, :].unsqueeze(1).to_broadcast([P, WINDOWS, F]),
                                    ALU.add).then_inc(s_xb, 1)
            dve.wait_ge(s_tot, 1)
            nc.vector.tensor_scalar(okay[:, :], bank[0][:, 0:1], 0.0, None, ALU.is_equal).then_inc(s_ctlf, 1)
            dve.wait_ge(flat_taken, 2 * RING * G)
            tmi = [wide[:, 2 * RING * SUPER + i * CHUNKS:2 * RING * SUPER + (i + 1) * CHUNKS].bitcast(I32) for i in range(2)]
            tmi.append(last_dst[:, 0:CHUNKS].bitcast(I32))
            sc, dc = src_ci[:, 0:CHUNKS], dst_ci[:, 0:CHUNKS]
            dve.wait_ge(s_constf, 8)
            dve.wait_ge(flat_turned, 2 * RING * G)
            nc.vector.tensor_copy(last_dst[:, 0:CHUNKS], dc).then_inc(s_key, 1)
            nc.vector.tensor_scalar(tmi[0], sc, 7, None, ALU.arith_shift_right).then_inc(s_key, 1)
            nc.vector.tensor_scalar(tmi[1], sc, P - 1, None, ALU.bitwise_and).then_inc(s_key, 1)
            dve.wait_ge(s_key, 3)
            nc.vector.tensor_scalar(src_c[:, 0:CHUNKS], tmi[1], -1.0, None, ALU.mult).then_inc(s_key, 1)
            nc.vector.memset(src_c[:, CHUNKS:], 0.0).then_inc(s_key, 1)
            dve.wait_ge(s_cntp, 4)
            ends_of, junk = last_dst[:, 0:PAIRS - 1], last_dst[:, PAIRS:2 * PAIRS - 1]
            for i in range(4):
                n = min(512, PAIRS - 1 - i * 512)
                nc.vector.tensor_copy(ends_of[:, i * 512:i * 512 + n], bank[1 + i][:, 0:n]).then_inc(s_zero, 1)
            dve.wait_ge(s_zero, 4)
            for c in range(CG):
                if c >= 1:
                    dve.wait_ge(s_cnt, c)
                nc.vector.tensor_scalar(junk, ends_of, thr[:, c:c + 1], None,
                                        ALU.is_lt, ALU.add, accum_out=cnt_f[:, c:c + 1]).then_inc(s_cnt, 1)
            dve.wait_ge(s_cnt, CG)
            dve.wait_ge(s_ctlf, 1)
            nc.vector.tensor_scalar(cnt_g[:, :], cnt_f[:, :], okay[:, :], None, ALU.mult).then_inc(s_cnt, 1)
            dve.wait_ge(s_key, 5)
            nc.vector.tensor_scalar(tmi[2], dc, SUBN - 1, None, ALU.bitwise_and).then_inc(s_key, 1)
            nc.vector.tensor_scalar(tmi[1], dc, 2, 10, ALU.arith_shift_right, ALU.logical_shift_left).then_inc(s_key, 1)
            dve.wait_ge(s_key, 7)
            nc.vector.tensor_tensor(dst_c[:, 0:CHUNKS], tmi[0], tmi[1], ALU.add).then_inc(s_key, 1)
            dve.wait_ge(s_key, 8)
            nc.vector.scalar_tensor_tensor(out=dst_c[:, 0:CHUNKS], in0=tmi[2], scalar=float(WINDOWS), in1=dst_c[:, 0:CHUNKS],
                                           op0=ALU.mult, op1=ALU.add).then_inc(s_key, 1)
            nc.vector.memset(dst_c[:, CHUNKS:], -1.0).then_inc(s_key, 1)
            nc.vector.tensor_copy(key_no, key_i[:, :]).then_inc(s_key, 1)
            dve.wait_ge(s_key, 11)
            ends = last_dst[:, 0:SUBS]
            dve.wait_ge(s_cntd, 32)
            nc.vector.scalar_tensor_tensor(out=ends, in0=sub_base[:, :], scalar=1.0 / 1024, in1=before_sub[:, 1:SUBS + 1],
                                           op0=ALU.mult, op1=ALU.add).then_inc(s_vis, 1)
            dve.wait_ge(s_vis, 1)
            nc.vector.tensor_scalar(last_dst[:, 3 * SUBS:3 * SUBS + DENSE], ends.rearrange("p (d u) -> p d u", u=P // SUBN)[:, :, P // SUBN - 1],
                                    VISITS - 0.5, None, ALU.is_lt, ALU.add, accum_out=dense_f[:, 0:1]).then_inc(s_vis, 1)
            dve.wait_ge(s_vis, 2)
            nc.vector.tensor_tensor(dense_f[:, 1:2], dense_f[:, 0:1], okay[:, :], ALU.mult).then_inc(s_vis, 1)
            dve.wait_ge(s_vis, 3)
            nc.vector.tensor_scalar(lim[:, :], dense_f[:, 1:2], float(P), None, ALU.mult).then_inc(s_vis, 1)
            dve.wait_ge(s_vis, 4)
            nc.vector.tensor_tensor(check2[:, 1:2], checks[:, 2:3], lim[0:ROWS, :], ALU.is_lt).then_inc(s_low, 1)
            for c in range(TV + 2):
                if c >= 2:
                    dve.wait_ge(s_vis, c + 3)
                junk = (1 + c % 2) * SUBS
                nc.vector.tensor_scalar(last_dst[0:ROWS, junk:junk + SUBS], ends[0:ROWS, :], vis[:, c:c + 1], None,
                                        ALU.is_lt, ALU.add, accum_out=sub[:, c:c + 1]).then_inc(s_vis, 1)
            n = TV + 6
            dve.wait_ge(s_vis, n)
            nc.vector.memset(sub[0:1, 0:1], -1.0).then_inc(s_vis, 1)
            dve.wait_ge(s_vis, n + 1)
            own = sub[:, 1:TV + 1]
            new, fin, low, par, code, to, change, other = (fields[:, i, :] for i in range(8))
            nc.vector.tensor_tensor(new, own, sub[:, 0:TV], ALU.is_gt).then_inc(s_vis, 1)
            nc.vector.tensor_tensor(change, sub[:, 2:TV + 2], own, ALU.is_gt).then_inc(s_vis, 1)
            nc.vector.tensor_scalar(low, own, float(SUBS - 1), None, ALU.min).then_inc(s_vis, 1)
            nc.vector.tensor_tensor(other, own, spare[:, :], ALU.subtract).then_inc(s_vis, 1)
            dve.wait_ge(s_vis, n + 5)
            nc.vector.tensor_copy(sub_n[:, :], low).then_inc(s_vis, 1)
            nc.vector.scalar_tensor_tensor(out=fin, in0=own, scalar=float(SUBS), in1=change, op0=ALU.is_lt, op1=ALU.mult).then_inc(s_vis, 1)
            dve.wait_ge(s_vis, n + 7)
            nc.vector.tensor_scalar(par_n[:, :], sub_n[:, :], 1, None, ALU.bitwise_and).then_inc(s_vis, 1)
            nc.vector.tensor_tensor(change, other, fin, ALU.mult).then_inc(s_vis, 1)
            dve.wait_ge(s_vis, n + 9)
            nc.vector.tensor_copy(par, par_n[:, :]).then_inc(s_vis, 1)
            nc.vector.tensor_tensor(to, change, spare[:, :], ALU.add).then_inc(s_vis, 1)
            dve.wait_ge(s_vis, n + 11)
            nc.vector.scalar_tensor_tensor(out=change, in0=par, scalar=-2.0, in1=new, op0=ALU.add, op1=ALU.mult).then_inc(s_vis, 1)
            dve.wait_ge(s_vis, n + 12)
            nc.vector.tensor_scalar(other, change, 2.0, 4.0, ALU.mult, ALU.add).then_inc(s_vis, 1)
            dve.wait_ge(s_vis, n + 13)
            nc.vector.tensor_tensor(code, other, par, ALU.add).then_inc(s_vis, 1)

            def nth(field, i):
                return field.rearrange("r (s i) -> r s i", i=PER)[:, :, i]

            def pack(out, a, b, unit):
                return nc.vector.scalar_tensor_tensor(out=packed[:, out, :], in0=b, scalar=float(unit), in1=a,
                                                      op0=ALU.mult, op1=ALU.add)

            nc.vector.tensor_copy(span_f[:, :, :], span_w[:, :, :]).then_inc(s_vis, 1)
            dve.wait_ge(s_vis, n + 15)
            pack(0, nth(low, 0), nth(low, 1), DIV).then_inc(s_vis, 1)
            pack(1, nth(to, 0), nth(to, 1), DIV).then_inc(s_vis, 1)
            pack(2, nth(code, 0), nth(code, 1), 8).then_inc(s_vis, 1)
            pack(3, span_f[:, :, 0], span_f[:, :, 1], P).then_inc(s_vis, 1)
            nc.vector.tensor_copy(words[:, 2, :], nth(low, 2)).then_inc(s_vis, 1)
            nc.vector.tensor_copy(words[:, 3, :], nth(to, 2)).then_inc(s_vis, 1)
            dve.wait_ge(s_vis, n + 21)
            pack(4, packed[:, 2, :], nth(code, 2), 64).then_inc(s_vis, 1)
            nc.vector.tensor_copy(words[:, 0:2, :], packed[:, 0:2, :]).then_inc(s_vis, 1)
            nc.vector.tensor_scalar(words[:, 4:6, :], words[:, 2:4, :], 20, None, ALU.logical_shift_left).then_inc(s_vis, 1)
            dve.wait_ge(s_vis, n + 24)
            pack(5, packed[:, 3, :], packed[:, 4, :], P * P).then_inc(s_vis, 1)
            by_super = tab_dve[:, 0:2 * RING].rearrange("r (s i) -> r s i", i=2)
            nc.vector.tensor_tensor(by_super[:, :, 0], words[:, 0, :], words[:, 4, :], ALU.bitwise_or).then_inc(s_vis, 1)
            nc.vector.tensor_copy(by_super[:, :, 1], packed[:, 3, :]).then_inc(s_vis, 1)
            nc.vector.tensor_tensor(tab_act[:, 0:RING], words[:, 0, :], words[:, 4, :], ALU.bitwise_or).then_inc(s_vis, 1)
            nc.vector.tensor_tensor(tab_sp[:, 0:RING], words[:, 1, :], words[:, 5, :], ALU.bitwise_or).then_inc(s_vis, 1)
            dve.wait_ge(s_vis, n + 29)
            nc.vector.tensor_copy(tab_pe[:, 0:RING], packed[:, 5, :]).then_inc(s_vis, 1)
            assert n + 30 == VIS
            dve.wait_ge(s_tot, 2)
            nc.vector.tensor_scalar(ctl_f[:, 0:1], bank[3][0:1, 0:1], float(TURNS - 2), None, ALU.min).then_inc(s_ctlf, 1)
            nc.vector.tensor_copy(ctl_f[:, 2:3], dense_f[0:1, 1:2]).then_inc(s_ctlf, 1)
            dve.wait_ge(s_ctlf, 3)
            nc.vector.tensor_scalar(ctl_f[:, 1:2], ctl_f[:, 0:1], -1.0, float(TURNS), ALU.mult, ALU.add).then_inc(s_ctlf, 1)
            dve.wait_ge(s_ctlf, 4)
            turns_f, dense_n_f = ctl_f[:, 1:2], ctl_f[:, 2:3]
            nc.vector.scalar_tensor_tensor(out=ctl_f[:, 5:6], in0=dense_n_f, scalar=2.0, in1=turns_f, op0=ALU.mult, op1=ALU.subtract).then_inc(s_ctlf, 1)
            nc.vector.tensor_tensor(ctl_f[:, 6:7], turns_f, dense_n_f, ALU.subtract).then_inc(s_ctlf, 1)
            dve.wait_ge(s_ctlf, 6)
            nc.vector.tensor_scalar(ctl_f[:, 7:8], ctl_f[:, 5:6], 0.0, None, ALU.max).then_inc(s_ctlf, 1)
            nc.vector.tensor_scalar(ctl_f[:, 8:9], ctl_f[:, 6:7], 0.0, None, ALU.max).then_inc(s_ctlf, 1)
            dve.wait_ge(s_ctlf, 8)
            nc.vector.tensor_tensor(ctl_f[:, 3:4], ctl_f[:, 7:8], turns_f, ALU.min).then_inc(s_ctlf, 1)
            nc.vector.tensor_tensor(ctl_f[:, 4:5], ctl_f[:, 8:9], dense_n_f, ALU.min).then_inc(s_ctlf, 1)
            dve.wait_ge(s_ctlf, 10)
            nc.vector.tensor_copy(ctl[:, :], ctl_f[:, 0:5]).then_inc(s_ctl, 1)
            dve.wait_ge(s_spand, 64)
            dve.wait_ge(s_zero, 5)
            dve.wait_ge(s_vis, VIS)
            dve.wait_ge(idx_taken, 2 * RING * G + 1)
            first_turn, hop_turns, dense_n, dense_1, dense_2 = control(dve)
            dve_turn = dve.alloc_register("dve_turn")
            dve_win = dve.alloc_register("dve_win")
            dve_after = dve.alloc_register("dve_after")

            def stage(t, s):
                return nc.vector.tensor_copy(idx[:, s * G:(s + 1) * G], src_all[:, bass.ds(t * (RING * G) + s * G, G)])

            dve_sub = dve.alloc_register("dve_sub")
            dve_chunk = dve.alloc_register("dve_chunk")

            def pair_rows(t, s, subs):
                for i in range(PER):
                    v, w = t * TV + (PER * s + i), (subs >> (10 * i)) & (DIV - 1)
                    wb = turn_of(dve, dve_sub, w, SUBS - 1)
                    chunk = turn_of(dve, dve_chunk, (v - wb) * 2, 2 * (PAIRS - 1))
                    dve.wait_ge(visit_done, v + 1)
                    for c in range(2):
                        at = ((PER * s + i) % HOTS) * 2 + c
                        if i < PER - LOWS:
                            nc.vector.tensor_scalar(low_hot[:, at * P:(at + 1) * P], key_no[:, 0:P], src_c[:, bass.ds(chunk + c, 1)], 0.0,
                                                    ALU.add, ALU.is_equal)
                        th = nc.vector.tensor_scalar(key_hot[:, at * SUBW:(at + 1) * SUBW], key_no, sub_base[:, bass.ds(wb, 1)],
                                                     dst_c[:, bass.ds(chunk + c, 1)], ALU.add, ALU.is_equal)
                    th.then_inc(pair_hot, 1)

            dve_second, dve_more, dve_at = (dve.alloc_register(f"dve_{n}") for n in ("second", "more", "at"))
            for r in (dve_second, dve_more):
                dve.reg_mov(r, 0)

            def one_hot(t, s, w, rows_of):
                d = dst_all[:, bass.ds(t * (RING * G) + s * G, G)].unsqueeze(2).to_broadcast([P, G, P])
                return nc.vector.scalar_tensor_tensor(
                    out=rows_of[s], in0=d, scalar=base[:, bass.ds(w, 1)],
                    in1=node[:, :].unsqueeze(1).to_broadcast([P, G, P]), op0=ALU.subtract, op1=ALU.is_equal)

            def one_hots(t, s, span_s):
                first, last = span_s
                one_hot(t, s, first, hot3).then_inc(hot_ready, 1)
                with dve.If(last > first):
                    one_hot(t, s, turn_of(dve, dve_at, first + 1, WINDOWS - 1), second3).then_inc(second_hot, 1)

            def accumulate(k, t, s, span_s, width):
                def add(w, n=1):
                    a = agg[:, bass.ds(w * FD, n * FD)].rearrange("p (w f) -> p w f", f=FD)[:, :, 0:width]
                    by = seg_ps[s % 2][:, 0:n * P].rearrange("p (w f) -> p w f", f=P)[:, :, 0:width]
                    return nc.vector.tensor_tensor(a, a, by, ALU.add)
                first, last = span_s
                dve.wait_ge(seg_done, k + 1)
                hold(dve, acc_done, k + 2)
                with dve.If(last > first):
                    dve.wait_ge(second_seg, dve.snap(dve_second) + 1)
                    dve.reg_add(dve_second, dve_second, 1)
                    add(turn_of(dve, dve_at, first, WINDOWS - 2), 2).then_inc(acc_done, 1)
                    with dve.If(last > first + 1):
                        hold(dve, acc_done, k + 3)
                        with dve.Fori(first + 1, last) as w:
                            n = dve.snap(dve_more)
                            at = turn_of(dve, dve_at, w + 1, WINDOWS - 1)
                            one_hot(t, s, at, hot3).then_inc(more_hot, 1)
                            dve.wait_ge(more_seg, n + 1)
                            add(at).then_inc(more_acc, 1)
                            dve.reg_add(dve_more, dve_more, 1)
                            hold(dve, more_acc, n + 2)
                with dve.Else():
                    add(first).then_inc(acc_done, 1)

            def combine(t, s, after=None):
                dve.wait_ge(gathered[s], t * (16 * G) + 16 * G)
                stage(t + 1 if after is None else after, s)
                dve.wait_ge(embedded, t * RING + (s + 2))
                nc.vector.tensor_tensor(msg3[s][:, :, 0:F], rows[:, s, :].rearrange("p (g f) -> p g f", f=F),
                                        emb_ps[s % 2][:, 0:G * F].rearrange("p (g f) -> p g f", f=F),
                                        ALU.add).then_inc(rows_free, 1)

            dve_windows = [[dve.alloc_register(f"dve_{n}{s}") for n in ("first", "last")] for s in range(RING)]

            def record(t, s):
                subs, word = table(dve, tab_dve, t, 2 * s, 2 * s + 2, DIV ** 3 - 1)
                return subs, windows_of(dve, dve_windows[s], word)

            subs, windows = record(0, 0)
            one_hots(0, 0, windows)
            combine(0, 0)
            pair_rows(0, 0, subs)

            def turn(t, last, final=False):
                row = table(dve, tab_dve, t, 2, 2 * RING, DIV ** 3 - 1)
                first = [dve.snap(r, min_val=0, max_val=WINDOWS - 1) for r in dve_windows[0]]
                recs = [(None, first)] + [(row[2 * s - 2], windows_of(dve, dve_windows[s], row[2 * s - 1])) for s in range(1, RING)]
                for s in range(RING):
                    if s < RING - 1 or not last:
                        tn, sn = (t, s + 1) if s < RING - 1 else (t + 1, 0)
                        subs, windows = recs[s + 1] if s < RING - 1 else record(tn, 0)
                        one_hots(tn, sn, windows)
                        combine(tn, sn, first_turn if last or (final and s == RING - 1) else None)
                        pair_rows(tn, sn, subs)
                    accumulate(t * RING + s, t, s, recs[s][1], FD)

            with dve.Fori(0, TURNS - 2) as t:
                turn(t, False)
            turn(TURNS - 2, False, final=True)
            turn(TURNS - 1, True)
            dve.wait_ge(acc_done, SUPERS + 2)
            nc.vector.tensor_scalar(span[:, :], span[:, :], ctl_f[:, 2:3], None, ALU.max).then_inc(s_cut, 1)
            dve.wait_ge(s_cut, 1)
            nc.vector.tensor_scalar(deg[:, :], agg3[:, :, F], 1.0, None, ALU.add).then_inc(s_deg, 1)
            dve.wait_ge(s_deg, 1)
            nc.vector.reciprocal(inv[:, :], deg[:, :]).then_inc(s_deg, 1)
            dve.wait_ge(s_dega, 1)
            nc.vector.reciprocal(dis[:, :], root[:, :]).then_inc(s_deg, 1)

            def add_h(j, nw):
                dve.wait_ge(m_T, j + 1)
                nc.vector.tensor_tensor(hs[:, 0:nw, :],
                                        agg[:, bass.ds(j * (GROUP * FD), nw * FD)].rearrange("p (w f) -> p w f", f=FD)[:, :, 0:F],
                                        xs[:, bass.ds(j * (GROUP * F), nw * F)].rearrange("p (w f) -> p w f", f=F),
                                        ALU.add).then_inc(m_h, 1)

            def copy_h(j, b, nw):
                dve.wait_ge(m_T, j + 2)
                dve.wait_ge(m_1, j + 1)
                nc.vector.tensor_copy(hT[b][:, 0:nw * P], bank[4][0:F, 0:nw * P]).then_inc(m_Tc, 1)

            dve.sem_inc(m_1, 2)
            dve.sem_inc(m_T, 1)
            add_h(0, GROUP)
            with dve.Fori(0, NORMS - 1) as i:
                for b in range(2):
                    add_h(i * 2 + (b + 1), GROUP)
                    copy_h(i * 2 + b, b, GROUP)
            add_h(GROUPS - 2, GROUP)
            copy_h(GROUPS - 3, 0, GROUP)
            add_h(GROUPS - 1, LAST)
            copy_h(GROUPS - 2, 1, GROUP)
            copy_h(GROUPS - 1, 0, LAST)
            for c in range(N // BN):
                dve.wait_ge(m_2a, 1 + min(GROUPS, -(-(c + 1) * BN // GN)))
                nc.vector.bn_stats(stats[:, c, :], h2T[:, c * BN:(c + 1) * BN]).then_inc(m_st, 1)
            dve.wait_ge(m_st, N // BN)
            nc.vector.bn_aggr(mv[:, :], stats2).then_inc(s_bn, 1)
            dve.wait_ge(s_bna, 1)
            nc.vector.reciprocal(bn[:, 1:2], bn[:, 0:1]).then_inc(s_bn, 1)
            dve.wait_ge(s_bn, 2)
            nc.vector.tensor_tensor(bn[:, 2:3], bn[:, 1:2], cols[:, 2:3], ALU.mult).then_inc(s_bn, 1)
            dve.wait_ge(s_bn, 3)
            nc.vector.tensor_tensor(bnt[:, :], mv[:, 0:1], bn[:, 2:3], ALU.mult).then_inc(s_bn, 1)
            dve.wait_ge(s_bn, 4)
            nc.vector.tensor_tensor(bn[:, 3:4], cols[:, 3:4], bnt[:, :], ALU.subtract).then_inc(s_bn, 1)

            def layer_norm(i, nw, m):
                xw = [xs[:, bass.ds(i * (NORM * F) + n * F, F)] for n in range(nw)]
                hold(dve, ln, m * CH + 1)
                for n in range(nw):
                    st = nc.vector.bn_stats(lst[:, n, :], xw[n])
                st.then_inc(ln, 1)
                hold(dve, ln, m * CH + 2)
                for n in range(nw):
                    ag = nc.vector.bn_aggr(lmv[:, n, :], lst[:, n, :])
                ag.then_inc(ln_v, 1)
                dve.wait_ge(ln_r, m + 1)
                nc.vector.reciprocal(lrs[:, :], lroot[:, :]).then_inc(ln, 1)
                dve.wait_ge(ln, m * CH + 3)
                for n in range(nw):
                    ts = nc.vector.tensor_scalar(xw[n], xw[n], lmv[:, n, 0:1], lrs[:, n:n + 1], ALU.subtract, ALU.mult)
                ts.then_inc(ln, 1)
                dve.wait_ge(ln, m * CH + 4)

            def first_norm(i, parts):
                nw = sum(parts)
                for b, n in enumerate(parts):
                    xw = xs[:, bass.ds(i * (NORM * F) + b * (GROUP * F), n * F)]
                    dve.wait_ge(b_T, i * 2 + (b + 3))
                    nc.vector.tensor_tensor(xw, xw, bank[4 + b][:, 0:n * F], ALU.add).then_inc(b_y, 1)
                hold(dve, b_y, i * 2 + (len(parts) + 2))
                layer_norm(i, nw, i)
                nc.vector.tensor_tensor(step_windows(agg, FD, i, nw)[:, :, 0:F], step_windows(xs, F, i, nw),
                                        dis[:, bass.ds(i * NORM, nw)].unsqueeze(2).to_broadcast([P, nw, F]),
                                        ALU.mult).then_inc(ln, 2)

            dve.sem_inc(ln, 1)
            dve.wait_ge(s_deg, 3)
            with dve.Fori(0, NORMS) as i:
                first_norm(i, (GROUP, GROUP))
            first_norm(NORMS, (LAST,))
            dve.wait_ge(ln, (NORMS + 1) * CH + 1)

            for h in range(2):
                dve.wait_ge(s_tab, 16 * (1 + (h + 1) * (NORMS + 1)))
                dve.wait_ge(s_x1, 16 * (NORMS + 1))
                nc.vector.tensor_copy(xs3, agg3[:, :, 0:F]).then_inc(s_gc, 1)

                def add_dense(w):
                    a = agg[:, bass.ds(turn_of(dve, dve_win, w, DENSE - 1) * FD, F)]
                    dve.wait_ge(dense_done, w + dense_n * h + 1)
                    nc.vector.tensor_tensor(a, a, bank[5][:, 0:F], ALU.add).then_inc(dense_acc, 1)

                def hop_turn(t):
                    to = turn_of(dve, dve_turn, t + first_turn)
                    dve.reg_mov(dve_after, first_turn)
                    with dve.If(hop_turns > t + 1):
                        dve.reg_mov(dve_after, t + first_turn + 1)
                    after = dve.snap(dve_after, min_val=0, max_val=TURNS - 1)
                    sp_t, sp_after = spans(dve, to), first_span(dve, after)
                    for s in range(RING):
                        one_hots(*((to, s + 1, sp_t[s + 1]) if s < RING - 1 else (after, 0, sp_after)))
                        dve.wait_ge(gathered[s], (t + hop_turns * h) * (16 * G) + 16 * G * (TURNS + 1))
                        accumulate((t + hop_turns * h) * RING + (SUPERS + s), to, s, sp_t[s], F)
                        stage(after, s).then_inc(rows_free, 1)

                if h == 0:
                    one_hots(first_turn, 0, first_span(dve, first_turn))
                with dve.If(dense_1 > 0):
                    with dve.Fori(0, dense_1) as t:
                        hop_turn(t)
                        add_dense(t)
                with dve.If(dense_2 > 0):
                    with dve.Fori(0, dense_2) as i:
                        hop_turn(dense_1 + i * 2)
                        hop_turn(dense_1 + i * 2 + 1)
                        add_dense(dense_1 + i)
                with dve.If(hop_turns > dense_1 + dense_2 * 2):
                    with dve.Fori(dense_1 + dense_2 * 2, hop_turns) as t:
                        hop_turn(t)
                with dve.If(dense_n > dense_1 + dense_2):
                    with dve.Fori(dense_1 + dense_2, dense_n) as w:
                        add_dense(w)
                        hold(dve, dense_acc, w + dense_n * h + 2)
                hold(dve, dense_acc, dense_n * (h + 1) + 1)
                hold(dve, acc_done, (hop_turns * (h + 1)) * RING + (SUPERS + 2))
                if h == 0:
                    def scale_sums(i, nw):
                        a = step_windows(agg, FD, i, nw)[:, :, 0:F]
                        nc.vector.tensor_tensor(a, a, inv[:, bass.ds(i * NORM, nw)].unsqueeze(2).to_broadcast([P, nw, F]),
                                                ALU.mult).then_inc(s_scaled, 1)

                    with dve.Fori(0, NORMS) as i:
                        scale_sums(i, NORM)
                    scale_sums(NORMS, NLAST)
                    dve.wait_ge(s_scaled, NORMS + 1)

            def second_norm(i, b, nw):
                dve.wait_ge(x1_in[b], i * 16 + 32)
                step = i * 2 + b
                for n in range(nw):
                    xw = xs[:, bass.ds(step * (NORM * F) + n * F, F)]
                    st = nc.vector.scalar_tensor_tensor(out=xw, in0=agg[:, bass.ds(step * (NORM * FD) + n * FD, F)],
                                                        scalar=dis[:, bass.ds(step * NORM + n, 1)], in1=xw,
                                                        op0=ALU.mult, op1=ALU.add)
                st.then_inc(b_y, 1)
                hold(dve, b_y, step + (GROUPS + 3))
                layer_norm(step, nw, step + (NORMS + 1))
                dve.sem_inc(ln, 2)
                dve.sem_inc(s_res, 1)

            with dve.Fori(0, NORMS // 2) as i:
                for b in range(2):
                    second_norm(i, b, NORM)
            second_norm(NORMS // 2, 0, NLAST)


_INS = ['x', 'src', 'dst', 'edge_attr_32', 'L0_gnn_We', 'L0_gnn_be', 'L0_gnn_W1', 'L0_gnn_b1',
        'L0_gnn_W2', 'L0_gnn_b2', 'L0_gnn_gamma', 'L0_gnn_beta']
_OUTS = [((12500, 96), 'float32')]


def kernel(**inputs):
    import numpy as _np
    import concourse.bacc as _bacc
    from concourse import mybir as _mybir
    from concourse.bass_utils import run_bass_kernel_spmd as _run

    nc = _bacc.Bacc("TRN2", target_bir_lowering=False, num_devices=1)
    arrays, args = {}, []
    for name in _INS:
        a = _np.ascontiguousarray(inputs[name])
        arrays[f"in_{name}_dram"] = a
        args.append(nc.dram_tensor(f"in_{name}_dram", a.shape, _mybir.dt.from_np(a.dtype), kind="ExternalInput").ap())
    for i, (shape, dtype) in enumerate(_OUTS):
        dt = _mybir.dt.from_np(_np.dtype(dtype))
        args.append(nc.dram_tensor(f"out_{i}_dram", shape, dt, kind="ExternalOutput").ap())
    gnn_kernel(nc, *args)
    r = _run(nc, [arrays], core_ids=[0])
    return r.results[0]["out_0_dram"]
```
